# Optimizing a Trainium2 kernel written in Bass

```python
import numpy as np
import jax
import jax.numpy as jnp

def _softmax(x, axis=-1):
    return jax.nn.softmax(x, axis=axis)

def _gelu(x):
    return jax.nn.gelu(x, approximate=True)

def _silu(x):
    return jax.nn.silu(x)

def _sigmoid(x):
    return jax.nn.sigmoid(x)

def _layernorm(x, axis=-1, eps=1e-05):
    m = jnp.mean(x, axis=axis, keepdims=True)
    v = jnp.var(x, axis=axis, keepdims=True)
    return (x - m) / jnp.sqrt(v + eps)

def _scatter_add(tgt, idx, src, axis=0):
    return tgt.at[idx].add(src)

def _segment_sum(src, seg, n):
    return jax.ops.segment_sum(src, seg, n)
kernel_name = 'mk_vit_tower_d1_tok_img768_r4_f95233'

def setup_inputs(seed: int=0):
    np.random.seed(seed)
    _w = jnp.asarray

    def _rec_inputs():
        import jax
        import jax.numpy as jnp
        _rk = jax.random.key(seed)
        x = jax.random.uniform(jax.random.fold_in(_rk, 1), (64, 3, 96, 96), jnp.float32, 0.0, 1)
        return x
    x = _rec_inputs()

    def _L0_tok_setup():
        import jax, jax.numpy as jnp
        import numpy as np
        B, C, H, W, P, D = (32, 3, 96, 96, 16, 192)
        N = H // P * (W // P)
        key = jax.random.key(seed)
        k0, k1, k2, k3 = jax.random.split(key, 4)
        x = jax.random.uniform(k0, (B, C, H, W), dtype=jnp.float32)
        proj_w = jax.random.normal(k1, (D, P * P * C), dtype=jnp.float32) * 0.02
        proj_b = jnp.zeros((D,), jnp.float32)
        cls_token = jax.random.normal(k2, (1, 1, D), dtype=jnp.float32)
        pos_embedding = jax.random.normal(k3, (1, N + 1, D), dtype=jnp.float32)
        return {'x': x, 'proj_w': proj_w, 'proj_b': proj_b, 'cls_token': cls_token, 'pos_embedding': pos_embedding}
    _L0_tok_all = _L0_tok_setup()
    _L0_tok_in = {k: v for k, v in _L0_tok_all.items() if k in ('proj_w', 'proj_b', 'cls_token', 'pos_embedding')}
    del _L0_tok_all

    def _L0_attn_setup():
        import jax, jax.numpy as jnp
        import numpy as np
        D = 192
        ORDER = 2
        K = 3
        MAXLEN = 512

        def _fft_conv(h, x, Bp):
            L = x.shape[-1]
            n = 2 * L
            h_f = jnp.fft.rfft(h, n=n, norm='forward')
            x_f = jnp.fft.rfft(x, n=n)
            y = jnp.fft.irfft(h_f * x_f, n=n, norm='forward')[..., :L]
            return y + x * Bp
        key = jax.random.key(seed)
        ks = jax.random.split(key, 8)
        Bsz, L = (4, 512)
        C = D * (ORDER + 1)
        u = jax.random.normal(ks[0], (Bsz, L, D), jnp.float32)
        W_lin = jax.random.normal(ks[1], (C, D), jnp.float32) / np.float32(np.sqrt(D))
        b_lin = jnp.zeros((C,), jnp.float32)
        conv_w = jax.random.normal(ks[2], (C, 1, K), jnp.float32) / np.float32(np.sqrt(K))
        conv_b = jnp.zeros((C,), jnp.float32)
        W_out = jax.random.normal(ks[3], (D, D), jnp.float32) / np.float32(np.sqrt(D))
        b_out = jnp.zeros((D,), jnp.float32)
        h_param = jax.random.normal(ks[4], (ORDER, D, MAXLEN), jnp.float32)
        win_b = jnp.zeros((1, D, 1), jnp.float32)
        min_decay = np.log(0.01) / 1.5
        max_decay = np.log(0.01) / 0.3
        alphas = jnp.linspace(min_decay, max_decay, D, dtype=jnp.float32)[None, :, None]
        Bmat = jax.random.normal(ks[5], (ORDER, 1, D, 1), jnp.float32)
        return dict(u=u, W_lin=W_lin, b_lin=b_lin, conv_w=conv_w, conv_b=conv_b, W_out=W_out, b_out=b_out, h_param=h_param, win_b=win_b, alphas=alphas, Bmat=Bmat)
    _L0_attn_all = _L0_attn_setup()
    _L0_attn_in = {k: v for k, v in _L0_attn_all.items() if k in ('W_lin', 'b_lin', 'conv_w', 'conv_b', 'W_out', 'b_out', 'h_param', 'win_b', 'alphas', 'Bmat')}
    del _L0_attn_all

    def _L0_ffn_setup():
        import jax, jax.numpy as jnp
        import numpy as np
        DEPTH = 11

        def _fff_forward(inputs, weights_in, weights_out, depth=DEPTH):
            B, S, _ = inputs.shape
            n_nodes = weights_in.shape[0]
            max_index = n_nodes - 1
            all_logits = jnp.einsum('bsd,nd->bsn', inputs, weights_in)

            def step(prev_idx, _):
                sel = jnp.clip(prev_idx, 0, max_index)
                logits = jnp.take_along_axis(all_logits, sel[..., None], axis=-1)[..., 0]
                new_idx = jnp.clip(2 * sel + 1 + (logits > 0).astype(sel.dtype), 0, max_index)
                return (new_idx, (logits, new_idx))
            idx0 = jnp.zeros((B, S), dtype=jnp.int32)
            _, (logits_seq, idx_seq) = jax.lax.scan(step, idx0, None, length=depth - 1)
            logits = jnp.concatenate([jnp.zeros((1, B, S), all_logits.dtype), logits_seq], axis=0)
            node_idx = jnp.concatenate([idx0[None], idx_seq], axis=0)
            act = jax.nn.gelu(logits, approximate=False)
            onehot = jax.nn.one_hot(node_idx, n_nodes, dtype=act.dtype)
            coeff = jnp.einsum('dbs,dbsn->bsn', act, onehot)
            return jnp.einsum('bsn,nd->bsd', coeff, weights_out)
        key = jax.random.key(seed)
        k1, k2, k3 = jax.random.split(key, 3)
        B, S, D = (4, 1024, 192)
        n_nodes = 2 * DEPTH - 1
        return {'inputs': jax.random.normal(k1, (B, S, D), dtype=jnp.float32), 'weights_in': jax.random.normal(k2, (n_nodes, D), dtype=jnp.float32), 'weights_out': jax.random.normal(k3, (n_nodes, D), dtype=jnp.float32)}
    _L0_ffn_all = _L0_ffn_setup()
    _L0_ffn_in = {k: v for k, v in _L0_ffn_all.items() if k in ('weights_in', 'weights_out')}
    del _L0_ffn_all
    return {'x': x, 'L0_tok_proj_w': _L0_tok_in['proj_w'], 'L0_tok_proj_b': _L0_tok_in['proj_b'], 'L0_tok_cls_token': _L0_tok_in['cls_token'], 'L0_tok_pos_embedding': _L0_tok_in['pos_embedding'], 'L0_attn_W_lin': _L0_attn_in['W_lin'], 'L0_attn_b_lin': _L0_attn_in['b_lin'], 'L0_attn_conv_w': _L0_attn_in['conv_w'], 'L0_attn_conv_b': _L0_attn_in['conv_b'], 'L0_attn_W_out': _L0_attn_in['W_out'], 'L0_attn_b_out': _L0_attn_in['b_out'], 'L0_attn_h_param': _L0_attn_in['h_param'], 'L0_attn_win_b': _L0_attn_in['win_b'], 'L0_attn_alphas': _L0_attn_in['alphas'], 'L0_attn_Bmat': _L0_attn_in['Bmat'], 'L0_ffn_weights_in': _L0_ffn_in['weights_in'], 'L0_ffn_weights_out': _L0_ffn_in['weights_out']}

def reference(x, L0_tok_proj_w, L0_tok_proj_b, L0_tok_cls_token, L0_tok_pos_embedding, L0_attn_W_lin, L0_attn_b_lin, L0_attn_conv_w, L0_attn_conv_b, L0_attn_W_out, L0_attn_b_out, L0_attn_h_param, L0_attn_win_b, L0_attn_alphas, L0_attn_Bmat, L0_ffn_weights_in, L0_ffn_weights_out):
    import jax
    import jax.numpy as jnp

    def _L0_tok_ref(x, proj_w, proj_b, cls_token, pos_embedding):
        import jax, jax.numpy as jnp
        import numpy as np
        B, C, H, W, P, D = (32, 3, 96, 96, 16, 192)
        N = H // P * (W // P)
        b, c, h, w = x.shape
        hp, wp = (h // P, w // P)
        patches = x.reshape(b, c, hp, P, wp, P).transpose(0, 2, 4, 1, 3, 5).reshape(b, hp * wp, c * P * P)
        tok = jnp.einsum('bnk,dk->bnd', patches, proj_w) + proj_b
        cls = jnp.broadcast_to(cls_token, (b, 1, cls_token.shape[-1]))
        z0 = jnp.concatenate([cls, tok], axis=1) + pos_embedding
        return z0

    def _L0_attn_ref(u, W_lin, b_lin, conv_w, conv_b, W_out, b_out, h_param, win_b, alphas, Bmat):
        import jax, jax.numpy as jnp
        import numpy as np
        D = 192
        ORDER = 2
        K = 3
        MAXLEN = 512

        def _fft_conv(h, x, Bp):
            L = x.shape[-1]
            n = 2 * L
            h_f = jnp.fft.rfft(h, n=n, norm='forward')
            x_f = jnp.fft.rfft(x, n=n)
            y = jnp.fft.irfft(h_f * x_f, n=n, norm='forward')[..., :L]
            return y + x * Bp
        Bsz, L, d = u.shape
        z = (u @ W_lin.T + b_lin).transpose(0, 2, 1)
        z = jax.lax.conv_general_dilated(z, conv_w, window_strides=(1,), padding=[(K - 1, K - 1)], feature_group_count=z.shape[1], dimension_numbers=('NCH', 'OIH', 'NCH'))[..., :L] + conv_b[None, :, None]
        xs = [z[:, i * d:(i + 1) * d] for i in range(ORDER)]
        v = z[:, ORDER * d:] + u.transpose(0, 2, 1)
        t = jnp.linspace(0.0, 1.0, MAXLEN, dtype=u.dtype)[None, None, :L]
        h = h_param[:, :, :L] * (jnp.exp(alphas * t) + win_b)
        h = h / jnp.sum(jnp.abs(h), axis=-2, keepdims=True)
        for i in range(ORDER):
            v = v + jax.nn.softmax(xs[i], axis=1) * _fft_conv(h[i][None], v, Bmat[i])
        v = v.transpose(0, 2, 1)
        return v + v @ W_out.T + b_out

    def _L0_ffn_ref(inputs, weights_in, weights_out):
        import jax, jax.numpy as jnp
        import numpy as np
        DEPTH = 11

        def _fff_forward(inputs, weights_in, weights_out, depth=DEPTH):
            B, S, _ = inputs.shape
            n_nodes = weights_in.shape[0]
            max_index = n_nodes - 1
            all_logits = jnp.einsum('bsd,nd->bsn', inputs, weights_in)

            def step(prev_idx, _):
                sel = jnp.clip(prev_idx, 0, max_index)
                logits = jnp.take_along_axis(all_logits, sel[..., None], axis=-1)[..., 0]
                new_idx = jnp.clip(2 * sel + 1 + (logits > 0).astype(sel.dtype), 0, max_index)
                return (new_idx, (logits, new_idx))
            idx0 = jnp.zeros((B, S), dtype=jnp.int32)
            _, (logits_seq, idx_seq) = jax.lax.scan(step, idx0, None, length=depth - 1)
            logits = jnp.concatenate([jnp.zeros((1, B, S), all_logits.dtype), logits_seq], axis=0)
            node_idx = jnp.concatenate([idx0[None], idx_seq], axis=0)
            act = jax.nn.gelu(logits, approximate=False)
            onehot = jax.nn.one_hot(node_idx, n_nodes, dtype=act.dtype)
            coeff = jnp.einsum('dbs,dbsn->bsn', act, onehot)
            return jnp.einsum('bsn,nd->bsd', coeff, weights_out)
        return _fff_forward(inputs, weights_in, weights_out)
    h = _L0_tok_ref(x, L0_tok_proj_w, L0_tok_proj_b, L0_tok_cls_token, L0_tok_pos_embedding)
    h = h + _L0_attn_ref(_layernorm(h, axis=-1), L0_attn_W_lin, L0_attn_b_lin, L0_attn_conv_w, L0_attn_conv_b, L0_attn_W_out, L0_attn_b_out, L0_attn_h_param, L0_attn_win_b, L0_attn_alphas, L0_attn_Bmat)
    h = h + _L0_ffn_ref(_layernorm(h, axis=-1), L0_ffn_weights_in, L0_ffn_weights_out)
    return h

_drawn_inputs = setup_inputs


def setup_inputs(seed=0):
    import zlib

    import numpy as np

    out = dict(_drawn_inputs(seed))
    spreads = {'L0_tok_proj_b': (0.0, 0.1),
     'L0_attn_b_lin': (0.0, 0.1),
     'L0_attn_conv_b': (0.0, 0.1),
     'L0_attn_b_out': (0.0, 0.1),
     'L0_attn_win_b': (0.0, 0.1)}
    factors = {}
    for name, (base, spread) in spreads.items():
        noise = np.random.default_rng([zlib.crc32(name.encode()), seed]).standard_normal(out[name].shape)
        drawn = base * np.exp(spread * noise) if base else spread * noise
        out[name] = jnp.asarray(drawn.astype(out[name].dtype))
    for name, factor in factors.items():
        out[name] = (out[name] * factor).astype(out[name].dtype)
    return out
```

```python
from contextlib import ExitStack

import numpy as np

import concourse.bass as bass
from concourse import mybir

F32 = mybir.dt.float32
ALU = mybir.AluOpType
ACT = mybir.ActivationFunctionType
AX_X = mybir.AxisListType.X

IMAGES = 64
CHANNELS_IN, SIDE, PATCH = 3, 96, 16
PATCHES = (SIDE // PATCH) ** 2
SEQ = PATCHES + 1
POS = 40
TILE_IMAGES = 3
ROWS = TILE_IMAGES * POS
TILES = -(-IMAGES // TILE_IMAGES)
SLOTS = TILES * TILE_IMAGES
D = 192
KDIM = CHANNELS_IN * PATCH * PATCH
KCH = KDIM // 128
GROUPS = 3
DG = D // GROUPS
ORDERS = 2
ZC = (ORDERS + 1) * D
ZCH = [(c, min(128, ZC - c)) for c in range(0, ZC, 128)]
EPS = 1e-5
MAXLEN = 512
NODES = 21
TREE = 31
BATCH = 4
STEPS = [list(range(t, min(t + BATCH, TILES))) for t in range(0, TILES, BATCH)]
BLK = 8
NBLK = DG // BLK
HALVES = [STEPS[0] + STEPS[1] + STEPS[2], STEPS[3] + STEPS[4] + STEPS[5]]


def build(nc, xT, wproj, posb, wlinA, wlinB, convw, wout, hraw, hpar, tconst, ident, groupsum, wffi, wffo, out):
    ctx = ExitStack()
    with ctx:
        def sb(name, shape):
            return ctx.enter_context(nc.sbuf_tensor(name, shape, F32))

        def sem(name):
            return ctx.enter_context(nc.semaphore(name))

        bank = [ctx.enter_context(nc.psum_tensor(f"bank{i}", [128, 512], F32)) for i in range(8)]

        ident_sb = sb("ident_sb", [128, 128])
        groupsum_sb = sb("groupsum_sb", [ROWS, ROWS])
        wproj_sb = sb("wproj_sb", [128, KCH, D])
        posb_sb = sb("posb_sb", [ROWS, 2, D])
        pos_sb = sb("pos_sb", [ROWS, D])
        wlinA_sb = sb("wlinA_sb", [128, ZC])
        wlinB_sb = sb("wlinB_sb", [65, ZC])
        convw_sb = sb("convw_sb", [128, len(ZCH), 4])
        wout_sb = sb("wout_sb", [65, GROUPS, D])
        wffi_sb = sb("wffi_sb", [128, 2, NODES])
        wffo_sb = sb("wffo_sb", [NODES, D])
        hpar_sb = sb("hpar_sb", [ROWS, 4, DG])
        tconst_sb = sb("tconst_sb", [ROWS, 3, POS])
        neghalf = sb("neghalf", [ROWS, BATCH])

        xbuf = sb("xbuf", [128, BATCH, KCH * ROWS])
        h = sb("h", [ROWS, TILES, D])
        u = sb("u", [ROWS, 2 * BATCH, D])
        stats = sb("stats", [ROWS, 2, 6])
        mv = sb("mv", [ROWS, TILES, 2])
        vareps = sb("vareps", [ROWS, BATCH])
        rstd = sb("rstd", [ROWS, TILES])
        uTA = sb("uTA", [128, BATCH * ROWS])
        uTB = sb("uTB", [65, BATCH * ROWS])
        zc = sb("zc", [128, len(ZCH), BATCH * ROWS])
        nmax = sb("nmax", [ROWS, TILES, ORDERS])
        esum = sb("esum", [ROWS, TILES, ORDERS])
        rsum = sb("rsum", [ROWS, TILES, ORDERS])
        stage = sb("stage", [ROWS, BATCH, GROUPS, ORDERS + 1, DG])
        X3 = sb("X3", [ROWS, SLOTS, ORDERS + 1, DG])
        toep = [sb(f"toep{i}", [ROWS, DG, ROWS]) for i in range(ORDERS)]
        filt1 = sb("filt1", [ROWS, DG, POS])
        prep = toep[1][:, :, :].rearrange("p a b -> p (a b)").rearrange("p (n a b) -> p n a b", n=3, b=POS)
        hfilt, env = prep[:, 0:2], prep[:, 2]
        norm = sb("norm", [ROWS, ORDERS, POS])
        rnorm = sb("rnorm", [ROWS, ORDERS, POS])
        xflat = xbuf[:, :, :].rearrange("p a b -> p (a b)")
        zflat = zc[:, :, :].rearrange("p a b -> p (a b)")
        ytmp = [zflat[0:ROWS, k * 512:(k + 1) * 512].rearrange("p (a b) -> p a b", a=BLK) for k in range(2)]
        VT = [xflat[0:65, k * 360:(k + 1) * 360] for k in range(2)]
        n2TA, n2TB = uTA, uTB
        tflat = toep[0][:, :, :].rearrange("p a b -> p (a b)")
        used = [0]

        def part(n):
            used[0] += n
            return tflat[:, used[0] - n:used[0]]

        act_ = [part(len(ts) * NODES).rearrange("p (t n) -> p t n", n=NODES) for ts in HALVES]
        sgn = [part(len(ts) * 15).rearrange("p (t n) -> p t n", n=15) for ts in HALVES]
        reach = [part(len(ts) * (TREE + 1)).rearrange("p (t n) -> p t n", n=TREE + 1) for ts in HALVES]
        coef = [part(len(ts) * (TREE + 1)).rearrange("p (t n) -> p t n", n=TREE + 1) for ts in HALVES]
        q = [part(len(ts) * 8).rearrange("p (t n) -> p t n", n=8) for ts in HALVES]
        last = [part(len(ts) * 6).rearrange("p (t n) -> p t n", n=6) for ts in HALVES]
        sums = [part(len(ts) * 2).rearrange("p (t n) -> p t n", n=2) for ts in HALVES]
        coefT = toep[1][:, :, :].rearrange("p a b -> p (a b)")[0:NODES, 0:BATCH * ROWS]

        w_first = sem("w_first")
        w_rest = sem("w_rest")
        w_filt = sem("w_filt")
        x_in = [sem(f"x_in{k}") for k in range(BATCH)]
        const_ready = sem("const_ready")
        ones_ready = sem("ones_ready")
        pos_ready = sem("pos_ready")
        tok_ready = sem("tok_ready")
        h_ready = sem("h_ready")
        st_ready = sem("st_ready")
        mv_ready = sem("mv_ready")
        ve_ready = sem("ve_ready")
        rstd_ready = sem("rstd_ready")
        u_ready = sem("u_ready")
        uT_ready = sem("uT_ready")
        uT_copied = sem("uT_copied")
        z_ready = sem("z_ready")
        tap2_ready = sem("tap2_ready")
        tap1_ready = sem("tap1_ready")
        zc_ready = sem("zc_ready")
        xs_ready = sem("xs_ready")
        v_ready = sem("v_ready")
        max_ready = sem("max_ready")
        exp_ready = sem("exp_ready")
        rsum_ready = sem("rsum_ready")
        gate_ready = sem("gate_ready")
        vtok_ready = sem("vtok_ready")
        moved = [sem(f"moved{k}") for k in range(2)]
        env_raw = sem("env_raw")
        env_exp = sem("env_exp")
        filt_step = sem("filt_step")
        norm_sum = sem("norm_sum")
        norm_all = sem("norm_all")
        norm_fix = sem("norm_fix")
        rnorm_ready = sem("rnorm_ready")
        toep_zero = sem("toep_zero")
        toep_in = [sem(f"toep_in{i}") for i in range(ORDERS)]
        y_ready = sem("y_ready")
        gated = sem("gated")
        v_added = sem("v_added")
        wout_ready = sem("wout_ready")
        vT_ready = sem("vT_ready")
        vT_copied = sem("vT_copied")
        o_ready = sem("o_ready")
        h2_ready = sem("h2_ready")
        st2_ready = sem("st2_ready")
        mv2_ready = sem("mv2_ready")
        ve2_ready = sem("ve2_ready")
        rstd2_ready = sem("rstd2_ready")
        n2_ready = sem("n2_ready")
        n2T_ready = sem("n2T_ready")
        n2T_copied = sem("n2T_copied")
        logit_ready = sem("logit_ready")
        gelu_ready = sem("gelu_ready")
        tree = sem("tree")
        coef_ready = sem("coef_ready")
        cT_ready = sem("cT_ready")
        cT_copied = sem("cT_copied")
        ffn_ready = sem("ffn_ready")
        out_ready = sem("out_ready")
        stored = sem("stored")

        PAIRS = [[ts[k], ts[k + 1]] for ts in STEPS for k in range(0, len(ts), 2)]
        MOVES = GROUPS * TILE_IMAGES

        def f_bank(p):
            return bank[3] if p < 6 else bank[p % 2]

        block = ctx.enter_context(nc.Block())

        @block.sync
        def _(sp):
            sp.dma_start(wproj_sb[:, :, :], wproj).then_inc(w_first, 16)

            def load(t):
                if t >= BATCH:
                    sp.wait_ge(tok_ready, t - BATCH + 1)
                sp.dma_start(xbuf[:, t % BATCH, :], xT[t]).then_inc(x_in[t % BATCH], 16)

            load(0)
            sp.dma_start(posb_sb[:, :, :], posb).then_inc(w_first, 16)
            sp.dma_start(ident_sb[:, :], ident).then_inc(w_rest, 16)
            for t in STEPS[0][1:]:
                load(t)
            sp.dma_start(hpar_sb[:, :, :], hpar).then_inc(w_filt, 16)
            sp.dma_start(tconst_sb[:, :, :], tconst).then_inc(w_filt, 16)
            for dst, src in ((wlinA_sb[:, :], wlinA), (wlinB_sb[:, :], wlinB), (convw_sb[:, :, :], convw)):
                sp.dma_start(dst, src).then_inc(w_rest, 16)
            for t in STEPS[1][:1]:
                load(t)
            sp.dma_start(hfilt, hraw).then_inc(w_filt, 16)
            for dst, src in ((groupsum_sb[:, :], groupsum), (wout_sb[:, :, :], wout),
                             (wffi_sb[:, :, :], wffi), (wffo_sb[:, :], wffo)):
                sp.dma_start(dst, src).then_inc(w_rest, 16)
            for t in STEPS[1][1:]:
                load(t)

            def move(p):
                sp.wait_ge(gate_ready, 2 * p + 2)
                sp.wait_ge(vtok_ready, 2 * p + 2)
                t0, s0 = 2 * p, (2 * p) % BATCH
                for j in range(TILE_IMAGES):
                    for g in range(GROUPS):
                        sp.dma_start(
                            X3[g * POS:(g + 1) * POS, TILE_IMAGES * t0 + j:TILE_IMAGES * (t0 + 1) + j + 1:TILE_IMAGES]
                            .rearrange("p b a d -> p b (a d)"),
                            stage[j * POS:(j + 1) * POS, s0:s0 + 2, g].rearrange("p t a d -> p t (a d)"),
                        ).then_inc(moved[p % 2], 16)

            def place(i):
                sp.wait_ge(filt_step, 9)
                sp.wait_ge(toep_zero, i + 1)
                src = hfilt[:, 0] if i == 0 else filt1[:, :, :]
                for g in range(GROUPS):
                    a, b = g * POS, (g + 1) * POS
                    sp.dma_start(toep[i][a:b, :, a:b], src[a:b]).then_inc(toep_in[i], 16)

            for g in range(len(STEPS)):
                if g + 2 < len(STEPS):
                    for t in STEPS[g + 2]:
                        load(t)
                if g == 4:
                    place(0)
                for k in range(0, len(STEPS[g]), 2):
                    move(STEPS[g][k] // 2)
            place(1)
            for p in range(len(PAIRS)):
                sp.wait_ge(out_ready, p + 1)
                sp.dma_start(out[:, 2 * p:2 * p + 2, :], h[:, 2 * p:2 * p + 2, :]).then_inc(stored, 16)
            sp.wait_ge(stored, 16 * len(PAIRS))

        @block.gpsimd
        def _(pool):
            nc.gpsimd.memset(neghalf[:, :], -0.5).then_inc(const_ready, 1)
            nc.gpsimd.memset(zc[:, :, :], 0.0).then_inc(const_ready, 1)

            def mult(o, a, b):
                return nc.gpsimd.tensor_tensor(o, a, b, ALU.mult)

            def add(o, a, b):
                return nc.gpsimd.tensor_tensor(o, a, b, ALU.add)

            full = [ROWS, DG, POS]

            def over_pos(ap):
                return ap.unsqueeze(2).broadcast_to(full)

            def over_ch(ap):
                return ap.unsqueeze(1).broadcast_to(full)

            pool.wait_ge(w_filt, 48)
            mult(env, over_pos(hpar_sb[:, 0]), over_ch(tconst_sb[:, 0])).then_inc(env_raw, 1)
            nc.gpsimd.memset(toep[0][:, :, :], 0.0).then_inc(toep_zero, 1)

            def rsqrt(g, var, mv_sem, ve_sem, out_sem):
                ts = STEPS[g]
                pool.wait_ge(mv_sem, ts[-1] + 1)
                nc.gpsimd.tensor_scalar(vareps[:, 0:len(ts)], mv[:, ts[0]:ts[-1] + 1, 1], EPS, None, ALU.add).then_inc(ve_sem, 1)
                pool.wait_ge(ve_sem, g + 1)
                nc.gpsimd.tensor_tensor(rstd[:, ts[0]:ts[-1] + 1], vareps[:, 0:len(ts)], neghalf[:, 0:len(ts)],
                                        ALU.pow).then_inc(out_sem, 1)

            pool.wait_ge(const_ready, 2)
            rsqrt(0, mv, mv_ready, ve_ready, rstd_ready)
            rsqrt(1, mv, mv_ready, ve_ready, rstd_ready)
            pool.wait_ge(env_exp, 1)
            add(env, env, over_pos(hpar_sb[:, 1])).then_inc(filt_step, 1)
            pool.wait_ge(filt_step, 1)
            mult(hfilt[:, 0], hfilt[:, 0], env).then_inc(filt_step, 1)
            mult(hfilt[:, 1], hfilt[:, 1], env).then_inc(filt_step, 1)

            def softmax_scale(t):
                pool.wait_ge(exp_ready, 2 * t + 2)
                pool.wait_ge(rsum_ready, t + 1)
                for i in range(ORDERS):
                    s = stage[:, t % BATCH, :, i, :]
                    ins = nc.gpsimd.tensor_scalar(s, s, rsum[:, t, i:i + 1], None, ALU.mult)
                ins.then_inc(gate_ready, 1)

            for g in range(len(STEPS)):
                if g + 2 < len(STEPS):
                    rsqrt(g + 2, mv, mv_ready, ve_ready, rstd_ready)
                for t in STEPS[g]:
                    softmax_scale(t)
                if g == 1:
                    pool.wait_ge(rnorm_ready, 1)
                    mult(hfilt[:, 0], hfilt[:, 0], over_ch(rnorm[:, 0])).then_inc(filt_step, 1)
                    mult(hfilt[:, 1], hfilt[:, 1], over_ch(rnorm[:, 1])).then_inc(filt_step, 1)
                if g == 2:
                    mult(env, over_pos(hpar_sb[:, 2]), over_ch(tconst_sb[:, 2])).then_inc(filt_step, 1)
                    pool.wait_ge(filt_step, 6)
                    add(hfilt[:, 0], hfilt[:, 0], env).then_inc(filt_step, 1)
                    pool.wait_ge(filt_step, 7)
                    mult(env, over_pos(hpar_sb[:, 3]), over_ch(tconst_sb[:, 2])).then_inc(filt_step, 1)
                    pool.wait_ge(filt_step, 8)
                    add(filt1[:, :, :], hfilt[:, 1], env).then_inc(filt_step, 1)
            pool.wait_ge(toep_in[0], 16 * GROUPS)
            pool.wait_ge(filt_step, 9)
            nc.gpsimd.memset(toep[1][:, :, :], 0.0).then_inc(toep_zero, 1)
            for g in range(len(STEPS)):
                rsqrt(g, mv, mv2_ready, ve2_ready, rstd2_ready)

        @block.scalar
        def _(act):
            def evac_T(src, pair, ready, copied, dstA, dstB):
                act.wait_ge(ready, pair + 1)
                c = (2 * pair % BATCH) * ROWS
                nc.scalar.copy(dstA[:, c:c + 2 * ROWS], src[0:128, 0:2 * ROWS]).then_inc(copied, 1)
                nc.scalar.copy(dstB[0:64, c:c + 2 * ROWS], src[0:64, 2 * ROWS:4 * ROWS]).then_inc(copied, 1)

            act.wait_ge(env_raw, 1)
            nc.scalar.activation(env, env, ACT.Exp).then_inc(env_exp, 1)
            act.wait_ge(w_rest, 16 * 8)
            act.wait_ge(const_ready, 2)
            nz = 0
            for g, ts in enumerate(STEPS):
                if g:
                    act.wait_ge(z_ready, 5 * g)
                for p in (ts[0] // 2, ts[-1] // 2)[:len(ts) // 2]:
                    evac_T(bank[2], p, uT_ready, uT_copied, uTA, uTB)
                imgs = len(ts) * TILE_IMAGES
                for c, (c0, m) in enumerate(ZCH):
                    act.wait_ge(z_ready, nz + 1)
                    if g and c == 0:
                        act.wait_ge(v_ready, ts[0])
                    dst = zc[0:m, c, 0:imgs * POS].rearrange("p (b l) -> p b l", l=POS)[:, :, 0:SEQ]
                    src = bank[4 + nz % 2][0:m, 0:imgs * SEQ].rearrange("p (b l) -> p b l", l=SEQ)
                    nc.scalar.activation(dst, src, ACT.Identity, bias=convw_sb[0:m, c, 3:4],
                                         scale=convw_sb[0:m, c, 2:3]).then_inc(tap2_ready, 1)
                    nz += 1
                for t in ts:
                    act.wait_ge(max_ready, t + 1)
                    if t >= BATCH:
                        p = (t - BATCH) // 2
                        act.wait_ge(moved[p % 2], 16 * MOVES * (p // 2 + 1))
                    for i in range(ORDERS):
                        nc.scalar.activation(
                            stage[:, t % BATCH, :, i, :],
                            bank[3 if t % 2 else 6][0:ROWS, i * D:(i + 1) * D].rearrange("p (g d) -> p g d", g=GROUPS),
                            ACT.Exp, bias=nmax[:, t, i:i + 1], accum_out=esum[:, t, i:i + 1]).then_inc(exp_ready, 1)

            def vT_evac(t):
                act.wait_ge(vT_ready, t + 1)
                if t >= 2:
                    act.wait_ge(o_ready, t - 1)
                dst = VT[t % 2][0:64, :].rearrange("p (g j l) -> p j g l", g=GROUPS, j=TILE_IMAGES)
                src = bank[t % 2][0:64, 0:3 * ROWS].rearrange("p (j g l) -> p j g l", g=GROUPS, j=TILE_IMAGES)
                nc.scalar.copy(dst, src).then_inc(vT_copied, 1)

            def n2_evac(g):
                for p in range(STEPS[g][0] // 2, STEPS[g][-1] // 2 + 1):
                    evac_T(bank[2], p, n2T_ready, n2T_copied, n2TA, n2TB)

            def gelu(k):
                act.wait_ge(logit_ready, k + 1)
                n = len(HALVES[k])
                nc.scalar.activation(act_[k], bank[3 if k == 0 else 6][0:ROWS, 0:n * NODES].rearrange("p (t n) -> p t n", n=NODES),
                                     ACT.Gelu).then_inc(gelu_ready, 1)

            def c_evac(g):
                act.wait_ge(cT_ready, g + 1)
                if g:
                    act.wait_ge(ffn_ready, 2 * g)
                n = len(STEPS[g]) * ROWS
                nc.scalar.copy(coefT[:, 0:n], bank[7][0:NODES, 0:n]).then_inc(cT_copied, 1)

            for g in range(len(STEPS)):
                for t in STEPS[g]:
                    vT_evac(t)
                if g >= 1:
                    n2_evac(g - 1)
                if g == 3:
                    gelu(0)
                if g == 5:
                    for gg in range(3):
                        c_evac(gg)
            n2_evac(5)
            gelu(1)
            for gg in range(3, 6):
                c_evac(gg)

        @block.vector
        def _(dve):
            def tt(o, a, b, op):
                return nc.vector.tensor_tensor(o, a, b, op)

            nc.vector.memset(uTB[64:65, :], 1.0).then_inc(ones_ready, 1)
            dve.wait_ge(w_first, 32)
            tt(pos_sb[:, :], posb_sb[:, 0], posb_sb[:, 1], ALU.add).then_inc(pos_ready, 1)
            dve.wait_ge(pos_ready, 1)

            def moments(t, h_sem, st_sem, mv_sem):
                dve.wait_ge(h_sem, t + 1)
                nc.vector.bn_stats(stats[:, t % 2], h[:, t]).then_inc(st_sem, 1)
                dve.wait_ge(st_sem, t + 1)
                nc.vector.bn_aggr(mv[:, t], stats[:, t % 2]).then_inc(mv_sem, 1)

            def embed(g):
                for t in STEPS[g]:
                    dve.wait_ge(tok_ready, t + 1)
                    tt(h[:, t], bank[t % 2][0:ROWS, 0:D], pos_sb[:, :], ALU.add).then_inc(h_ready, 1)
                    moments(t, h_ready, st_ready, mv_ready)

            def normalise(g, rstd_sem, out_sem):
                dve.wait_ge(rstd_sem, g + 1)
                for t in STEPS[g]:
                    nc.vector.tensor_scalar(u[:, t % (2 * BATCH)], h[:, t], mv[:, t, 0:1], rstd[:, t:t + 1],
                                            ALU.subtract, ALU.mult).then_inc(out_sem, 1)

            embed(0)
            normalise(0, rstd_ready, u_ready)
            embed(1)
            normalise(1, rstd_ready, u_ready)
            nz = 0
            for g, ts in enumerate(STEPS):
                imgs = len(ts) * TILE_IMAGES
                for c, (c0, m) in enumerate(ZCH):
                    dst = zc[0:m, c, 0:imgs * POS].rearrange("p (b l) -> p b l", l=POS)
                    src = bank[4 + nz % 2][0:m, 0:imgs * SEQ].rearrange("p (b l) -> p b l", l=SEQ)
                    dve.wait_ge(tap2_ready, nz + 1)
                    nc.vector.scalar_tensor_tensor(dst[:, :, 1:SEQ], src[:, :, 0:SEQ - 1], convw_sb[0:m, c, 1:2],
                                                   dst[:, :, 1:SEQ], ALU.mult, ALU.add).then_inc(tap1_ready, 1)
                    dve.wait_ge(tap1_ready, nz + 1)
                    nc.vector.scalar_tensor_tensor(dst[:, :, 2:SEQ], src[:, :, 0:SEQ - 2], convw_sb[0:m, c, 0:1],
                                                   dst[:, :, 2:SEQ], ALU.mult, ALU.add).then_inc(zc_ready, 1)
                    nz += 1
                if g + 2 < len(STEPS):
                    embed(g + 2)
                for t in ts:
                    dve.wait_ge(xs_ready, t + 1)
                    nc.vector.tensor_reduce(nmax[:, t, :],
                                            bank[3 if t % 2 else 6][0:ROWS, 0:2 * D].rearrange("p (a d) -> p a d", a=2),
                                            AX_X, ALU.max, negate=True).then_inc(max_ready, 1)
                    dve.wait_ge(v_ready, t + 1)
                    if t >= BATCH:
                        p = (t - BATCH) // 2
                        dve.wait_ge(moved[p % 2], 16 * MOVES * (p // 2 + 1))
                    tt(stage[:, t % BATCH, :, ORDERS, :],
                       bank[7][0:ROWS, 0:D].rearrange("p (g d) -> p g d", g=GROUPS),
                       u[:, t % (2 * BATCH)].rearrange("p (g d) -> p g d", g=GROUPS), ALU.add).then_inc(vtok_ready, 1)
                    dve.wait_ge(exp_ready, 2 * t + 2)
                    nc.vector.reciprocal(rsum[:, t, :], esum[:, t, :]).then_inc(rsum_ready, 1)
                if g + 2 < len(STEPS):
                    dve.wait_ge(vtok_ready, ts[-1] + 1)
                    normalise(g + 2, rstd_ready, u_ready)
                if g == 0:
                    dve.wait_ge(filt_step, 3)
                    nc.vector.tensor_reduce(norm[:, :, :], hfilt.rearrange("p i d l -> p i l d"), AX_X, ALU.add,
                                            apply_absolute_value=True).then_inc(norm_sum, 1)
                if g == 1:
                    dve.wait_ge(norm_all, 1)
                    tt(norm[:, :, :], bank[3][0:ROWS, 2 * D:2 * D + 2 * POS].rearrange("p (i l) -> p i l", i=2),
                       tconst_sb[:, 1].unsqueeze(1).broadcast_to([ROWS, ORDERS, POS]), ALU.add).then_inc(norm_fix, 1)
                    dve.wait_ge(norm_fix, 1)
                    nc.vector.reciprocal(rnorm[:, :, :], norm[:, :, :]).then_inc(rnorm_ready, 1)

            for g in range(GROUPS):
                tt(wout_sb[0:DG, g, g * DG:(g + 1) * DG], wout_sb[0:DG, g, g * DG:(g + 1) * DG],
                   ident_sb[0:DG, 0:DG], ALU.add).then_inc(wout_ready, 1)
            for k in range(2):
                nc.vector.memset(VT[k][64:65, :], 1.0).then_inc(wout_ready, 1)

            n = 0
            for i in range(ORDERS):
                for k in range(NBLK):
                    dve.wait_ge(y_ready, n + 1)
                    gate = X3[:, 0:IMAGES, i, k * BLK:(k + 1) * BLK].rearrange("p b d -> p d b")
                    v = X3[:, 0:IMAGES, ORDERS, k * BLK:(k + 1) * BLK].rearrange("p b d -> p d b")
                    y = bank[[0, 1, 4, 5][n % 4]][0:ROWS, :].rearrange("p (d b) -> p d b", d=BLK)
                    tt(ytmp[n % 2], y, gate, ALU.mult).then_inc(gated, 1)
                    dve.wait_ge(gated, n + 1)
                    tt(v, v, ytmp[n % 2], ALU.add).then_inc(v_added, 1)
                    n += 1

            def residual(ts):
                for t in ts:
                    dve.wait_ge(o_ready, t + 1)
                    tt(h[:, t], bank[4 + t % 2][0:ROWS, 0:D], h[:, t], ALU.add).then_inc(h2_ready, 1)
                    moments(t, h2_ready, st2_ready, mv2_ready)

            steps = [0]

            def link(ins):
                ins.then_inc(tree, 1)
                steps[0] += 1
                dve.wait_ge(tree, steps[0])

            def walk(k):
                ts = HALVES[k]
                a, s, r, c, qq = act_[k], sgn[k], reach[k], coef[k], q[k]
                dve.wait_ge(gelu_ready, k + 1)
                logits = bank[3 if k == 0 else 6][0:ROWS, 0:len(ts) * NODES].rearrange("p (t n) -> p t n", n=NODES)
                link(nc.vector.tensor_scalar(s, logits[:, :, 0:15], 0.0, None, ALU.is_gt))
                nc.vector.tensor_copy(r[:, :, 2:3], s[:, :, 0:1])
                nc.vector.tensor_scalar(r[:, :, 1:2], s[:, :, 0:1], -1.0, 1.0, ALU.mult, ALU.add)
                link(tt(c[:, :, 2:3], a[:, :, 0:1], s[:, :, 0:1], ALU.mult))
                link(tt(c[:, :, 1:2], a[:, :, 0:1], c[:, :, 2:3], ALU.subtract))
                for lo, hi in ((1, 3), (3, 7), (7, 15)):
                    w = hi - lo
                    right = slice(2 * lo + 2, 2 * hi + 1, 2)
                    left = slice(2 * lo + 1, 2 * hi, 2)
                    tt(r[:, :, right], r[:, :, lo:hi], s[:, :, lo:hi], ALU.mult)
                    link(tt(qq[:, :, 0:w], r[:, :, lo:hi], a[:, :, lo:hi], ALU.mult))
                    tt(r[:, :, left], r[:, :, lo:hi], r[:, :, right], ALU.subtract)
                    link(tt(c[:, :, right], qq[:, :, 0:w], s[:, :, lo:hi], ALU.mult))
                    link(tt(c[:, :, left], qq[:, :, 0:w], c[:, :, right], ALU.subtract))
                nl = NODES - 1
                nc.vector.tensor_reduce(sums[k][:, :, 0:1], c[:, :, nl:TREE], AX_X, ALU.add)
                link(nc.vector.tensor_reduce(sums[k][:, :, 1:2], r[:, :, nl:TREE], AX_X, ALU.add))
                link(nc.vector.tensor_copy(r[:, :, nl:nl + 1], sums[k][:, :, 1:2]))
                link(tt(last[k], r[:, :, 15:NODES], a[:, :, 15:NODES], ALU.mult))
                link(nc.vector.tensor_reduce(sums[k][:, :, 1:2], last[k], AX_X, ALU.add))
                link(tt(sums[k][:, :, 0:1], sums[k][:, :, 0:1], sums[k][:, :, 1:2], ALU.add))
                link(nc.vector.scalar_tensor_tensor(c[:, :, nl:nl + 1], a[:, :, nl:nl + 1], 5.0,
                                                    sums[k][:, :, 0:1], ALU.mult, ALU.add))
                nc.vector.memset(c[:, :, 0:1], 0.0).then_inc(coef_ready, 1)

            def finish(k):
                for p in range(HALVES[k][0] // 2, HALVES[k][-1] // 2 + 1):
                    dve.wait_ge(ffn_ready, p + 1)
                    tt(h[:, 2 * p:2 * p + 2].rearrange("p t d -> p (t d)"), f_bank(p)[0:ROWS, 0:2 * D],
                       h[:, 2 * p:2 * p + 2].rearrange("p t d -> p (t d)"), ALU.add).then_inc(out_ready, 1)

            for g in range(len(STEPS)):
                residual(STEPS[g][:1])
                if g >= 1:
                    if g >= 3:
                        dve.wait_ge(n2T_ready, STEPS[g - 3][-1] // 2 + 1)
                    normalise(g - 1, rstd2_ready, n2_ready)
                residual(STEPS[g][1:])
                if g == 3:
                    walk(0)
            normalise(5, rstd2_ready, n2_ready)
            finish(0)
            walk(1)
            finish(1)

        @block.tensor
        def _(pe):
            mm = nc.tensor.matmul

            def embed(g):
                for t in STEPS[g]:
                    pe.wait_ge(x_in[t % BATCH], 16 * (t // BATCH + 1))
                    if t >= 2:
                        pe.wait_ge(h_ready, t - 1)
                    for c in range(KCH):
                        ins = mm(bank[t % 2][0:ROWS, 0:D], xbuf[:, t % BATCH, c * ROWS:(c + 1) * ROWS],
                                 wproj_sb[:, c, :], start=(c == 0), stop=(c == KCH - 1))
                    ins.then_inc(tok_ready, 1)

            def turn(g, src_sem, ready, copied):
                for p in range(STEPS[g][0] // 2, STEPS[g][-1] // 2 + 1):
                    pe.wait_ge(src_sem, 2 * p + 2)
                    if p:
                        pe.wait_ge(copied, 2 * p)
                    for k in range(2):
                        s = u[:, (2 * p + k) % (2 * BATCH), :]
                        nc.tensor.transpose(bank[2][0:128, k * ROWS:(k + 1) * ROWS], s[:, 0:128], ident_sb[0:ROWS, 0:ROWS])
                    for k in range(2):
                        s = u[:, (2 * p + k) % (2 * BATCH), :]
                        ins = nc.tensor.transpose(bank[2][0:64, (2 + k) * ROWS:(3 + k) * ROWS], s[:, 128:D],
                                                  ident_sb[0:ROWS, 0:ROWS])
                    ins.then_inc(ready, 1)

            pe.wait_ge(w_first, 32)
            embed(0)
            embed(1)
            pe.wait_ge(w_rest, 16 * 8)
            pe.wait_ge(const_ready, 2)
            pe.wait_ge(ones_ready, 1)
            nz = 0
            for g, ts in enumerate(STEPS):
                turn(g, u_ready, uT_ready, uT_copied)
                imgs = len(ts) * TILE_IMAGES
                pe.wait_ge(uT_copied, ts[-1] + 1)
                for c, (c0, m) in enumerate(ZCH):
                    if nz >= 2:
                        pe.wait_ge(zc_ready, nz - 1)
                    dst = bank[4 + nz % 2][0:m, 0:imgs * SEQ].rearrange("p (b l) -> p b l", l=SEQ)
                    for w, src, rows, a in ((wlinA_sb, uTA, 128, True), (wlinB_sb, uTB, 65, False)):
                        rhs = src[0:rows, 0:imgs * POS].rearrange("p (b l) -> p b l", l=POS)[:, :, 0:SEQ]
                        ins = mm(dst, w[0:rows, c0:c0 + m], rhs, start=a, stop=not a)
                    ins.then_inc(z_ready, 1)
                    nz += 1
                if g + 2 < len(STEPS):
                    embed(g + 2)
                pe.wait_ge(zc_ready, nz)
                for t in ts:
                    b = bank[3 if t % 2 else 6]
                    if t >= 2:
                        pe.wait_ge(exp_ready, 2 * (t - 1))
                    cols = slice((t % BATCH) * ROWS, (t % BATCH + 1) * ROWS)
                    for c in range(3):
                        ins = nc.tensor.transpose(b[0:ROWS, c * 128:(c + 1) * 128], zc[:, c, cols], ident_sb[:, :])
                    ins.then_inc(xs_ready, 1)
                    if t >= 1:
                        pe.wait_ge(vtok_ready, t)
                    nc.tensor.transpose(bank[7][0:ROWS, 0:128], zc[:, 3, cols], ident_sb[:, :])
                    nc.tensor.transpose(bank[7][0:ROWS, 128:D], zc[0:64, 4, cols],
                                        ident_sb[0:64, 0:64]).then_inc(v_ready, 1)
                if g == 0:
                    pe.wait_ge(norm_sum, 1)
                    pe.wait_ge(exp_ready, 2 * len(ts))
                    mm(bank[3][0:ROWS, 2 * D:2 * D + 2 * POS], groupsum_sb[:, :],
                       norm[:, :, :].rearrange("p i l -> p (i l)"), start=True, stop=True).then_inc(norm_all, 1)

            for k in range(2):
                n_pairs = len([p for p in range(len(PAIRS)) if p % 2 == k])
                pe.wait_ge(moved[k], 16 * MOVES * n_pairs)
            n = 0
            for i in range(ORDERS):
                pe.wait_ge(toep_in[i], 16 * GROUPS)
                for k in range(NBLK):
                    if n >= 4:
                        pe.wait_ge(gated, n - 3)
                    if i:
                        pe.wait_ge(v_added, k + 1)
                    for j in range(BLK):
                        d = k * BLK + j
                        ins = mm(bank[[0, 1, 4, 5][n % 4]][0:ROWS, j * IMAGES:(j + 1) * IMAGES], toep[i][:, d, :],
                                 X3[:, 0:IMAGES, ORDERS, d], start=True, stop=True)
                    ins.then_inc(y_ready, 1)
                    n += 1

            pe.wait_ge(v_added, n)
            pe.wait_ge(wout_ready, 5)

            def v_turn(t):
                if t >= 2:
                    pe.wait_ge(vT_copied, t - 1)
                for j in range(TILE_IMAGES):
                    ins = nc.tensor.transpose(bank[t % 2][0:64, j * ROWS:(j + 1) * ROWS],
                                              X3[:, TILE_IMAGES * t + j, ORDERS, :], ident_sb[0:ROWS, 0:ROWS])
                ins.then_inc(vT_ready, 1)

            def project(t):
                pe.wait_ge(vT_copied, t + 1)
                if t >= 2:
                    pe.wait_ge(h2_ready, t - 1)
                for g in range(GROUPS):
                    rows = 65 if g == 0 else 64
                    w = VT[t % 2][0:rows, g * ROWS:(g + 1) * ROWS]
                    ins = mm(bank[4 + t % 2][0:ROWS, 0:D], w, wout_sb[0:rows, g, :],
                             start=(g == 0), stop=(g == GROUPS - 1))
                ins.then_inc(o_ready, 1)

            def logits(g):
                turn(g, n2_ready, n2T_ready, n2T_copied)
                pe.wait_ge(n2T_copied, STEPS[g][-1] + 1)
                half = 0 if g < 3 else 1
                for t in STEPS[g]:
                    o = (t - HALVES[half][0]) * NODES
                    dst = bank[3 if half == 0 else 6][0:ROWS, o:o + NODES]
                    c = (t % BATCH) * ROWS
                    mm(dst, n2TA[:, c:c + ROWS], wffi_sb[:, 0, :], start=True, stop=False)
                    ins = mm(dst, n2TB[0:64, c:c + ROWS], wffi_sb[0:64, 1, :], start=False, stop=True)
                if g in (2, 5):
                    ins.then_inc(logit_ready, 1)

            def tree_out(g):
                ts = STEPS[g]
                half = 0 if g < 3 else 1
                pe.wait_ge(coef_ready, half + 1)
                if g:
                    pe.wait_ge(cT_copied, g)
                for n_, t in enumerate(ts):
                    ins = nc.tensor.transpose(bank[7][0:NODES, n_ * ROWS:(n_ + 1) * ROWS],
                                              coef[half][:, t - HALVES[half][0], 0:NODES], ident_sb[0:ROWS, 0:ROWS])
                ins.then_inc(cT_ready, 1)
                pe.wait_ge(cT_copied, g + 1)
                for k in range(0, len(ts), 2):
                    p = ts[k] // 2
                    if p < 6 and p:
                        pe.wait_ge(out_ready, p)
                    if p >= 8:
                        pe.wait_ge(out_ready, p - 1)
                    for m in range(2):
                        ins = mm(f_bank(p)[0:ROWS, m * D:(m + 1) * D], coefT[:, (k + m) * ROWS:(k + m + 1) * ROWS],
                                 wffo_sb[:, :], start=True, stop=True)
                    ins.then_inc(ffn_ready, 1)

            for g, ts in enumerate(STEPS):
                for t in ts:
                    v_turn(t)
                    if t:
                        project(t - 1)
                if g == len(STEPS) - 1:
                    project(TILES - 1)
                if g >= 1:
                    logits(g - 1)
            for g in range(3):
                tree_out(g)
            logits(5)
            for g in range(3, len(STEPS)):
                tree_out(g)


_SHAPE_OUT = [ROWS, TILES, D]


def _laid_out(i):
    a = {k: np.asarray(v) for k, v in i.items()}
    side = SIDE // PATCH
    f = np.float32
    p = a["x"].reshape(IMAGES, CHANNELS_IN, side, PATCH, side, PATCH).transpose(0, 2, 4, 1, 3, 5)
    x = np.zeros((SLOTS, POS, KDIM), f)
    x[:IMAGES, 1:SEQ] = p.reshape(IMAGES, PATCHES, KDIM)
    xT = x.reshape(TILES, ROWS, KCH, 128).transpose(0, 3, 2, 1).reshape(TILES, 128, KCH * ROWS)
    wproj = a["L0_tok_proj_w"].T.reshape(KCH, 128, D).transpose(1, 0, 2)
    posb = np.zeros((TILE_IMAGES, POS, 2, D), f)
    posb[:, :SEQ, 0] = a["L0_tok_pos_embedding"][0]
    posb[:, 0, 1] = a["L0_tok_cls_token"][0, 0]
    posb[:, 1:SEQ, 1] = a["L0_tok_proj_b"]
    wl = a["L0_attn_W_lin"].T
    wlinB = np.zeros((65, ZC), f)
    wlinB[:64], wlinB[64] = wl[128:], a["L0_attn_b_lin"]
    cw = np.zeros((len(ZCH) * 128, 4), f)
    cw[:ZC, 0:3], cw[:ZC, 3] = a["L0_attn_conv_w"][:, 0], a["L0_attn_conv_b"]
    convw = cw.reshape(len(ZCH), 128, 4).transpose(1, 0, 2)
    wout = np.zeros((65, GROUPS, D), f)
    wout[:64] = a["L0_attn_W_out"].T.reshape(GROUPS, DG, D).transpose(1, 0, 2)
    wout[64, 0] = a["L0_attn_b_out"]
    hraw = np.zeros((GROUPS, POS, ORDERS, DG, POS), f)
    hp = a["L0_attn_h_param"][:, :, :SEQ].reshape(ORDERS, GROUPS, DG, SEQ).transpose(1, 0, 2, 3)
    tau = np.zeros((GROUPS, POS, POS), f)
    unused = np.ones((GROUPS, POS, POS), f)
    diag = np.zeros((GROUPS, POS, POS), f)
    t = (np.arange(MAXLEN, dtype=f) / f(MAXLEN - 1)).astype(f)
    for m in range(SEQ):
        hraw[:, m, :, :, m:SEQ] = hp[..., :SEQ - m]
        tau[:, m, m:SEQ] = t[:SEQ - m]
        unused[:, m, m:SEQ] = 0
        diag[:, m, m] = 1
    tconst = np.stack([tau, unused, diag], 2).reshape(ROWS, 3, POS)
    hpar = np.zeros((GROUPS, POS, 4, DG), f)
    hpar[:, :, 0] = a["L0_attn_alphas"].reshape(GROUPS, 1, DG)
    hpar[:, :, 1] = a["L0_attn_win_b"].reshape(GROUPS, 1, DG)
    for o in range(ORDERS):
        hpar[:, :, 2 + o] = a["L0_attn_Bmat"][o].reshape(GROUPS, 1, DG)
    groupsum = np.tile(np.eye(POS, dtype=f), (GROUPS, GROUPS))
    wi = np.zeros((256, NODES), f)
    wi[:D] = a["L0_ffn_weights_in"].T
    wffi = wi.reshape(2, 128, NODES).transpose(1, 0, 2)
    return dict(xT=xT, wproj=wproj, posb=posb.reshape(ROWS, 2, D), wlinA=wl[:128], wlinB=wlinB, convw=convw,
                wout=wout, hraw=hraw.reshape(ROWS, ORDERS, DG, POS), hpar=hpar.reshape(ROWS, 4, DG), tconst=tconst,
                ident=np.eye(128, dtype=f), groupsum=groupsum, wffi=wffi, wffo=a["L0_ffn_weights_out"])


def kernel(**inputs):
    import concourse.bacc as bacc
    from concourse.bass_utils import run_bass_kernel_spmd

    nc = bacc.Bacc("TRN2", target_bir_lowering=False, num_devices=1)
    arrays, args = {}, []
    for name, a in _laid_out(inputs).items():
        a = np.ascontiguousarray(a)
        arrays[f"in_{name}"] = a
        args.append(nc.dram_tensor(f"in_{name}", a.shape, F32, kind="ExternalInput").ap())
    out = nc.dram_tensor("out_rows", _SHAPE_OUT, F32, kind="ExternalOutput").ap()
    build(nc, *args, out)
    r = run_bass_kernel_spmd(nc, [arrays], core_ids=[0])
    rows = r.results[0]["out_rows"].reshape(TILE_IMAGES, POS, TILES, D).transpose(2, 0, 1, 3)
    return rows.reshape(SLOTS, POS, D)[:IMAGES, :SEQ]
```

```python
from contextlib import ExitStack

import numpy as np

import concourse.bass as bass
from concourse import mybir

F32 = mybir.dt.float32
ALU = mybir.AluOpType
ACT = mybir.ActivationFunctionType
AX_X = mybir.AxisListType.X

IMAGES = 64
CHANNELS_IN, SIDE, PATCH = 3, 96, 16
PATCHES = (SIDE // PATCH) ** 2
SEQ = PATCHES + 1
POS = 40
TILE_IMAGES = 3
ROWS = TILE_IMAGES * POS
TILES = -(-IMAGES // TILE_IMAGES)
SLOTS = TILES * TILE_IMAGES
D = 192
KDIM = CHANNELS_IN * PATCH * PATCH
KCH = KDIM // 128
GROUPS = 3
DG = D // GROUPS
ORDERS = 2
ZC = (ORDERS + 1) * D
ZCH = [(c, min(128, ZC - c)) for c in range(0, ZC, 128)]
EPS = 1e-5
MAXLEN = 512
NODES = 21
TREE = 31
BATCH = 4
STEPS = [list(range(t, min(t + BATCH, TILES))) for t in range(0, TILES, BATCH)]
COPIES = 10
BLK = 8
NBLK = DG // BLK
LATE = 4
HALVES = [sum(STEPS[:LATE], []), sum(STEPS[LATE:], [])]


def build(nc, xT, wproj, posb, wlinA, wlinB, convw, woutA, woutB, filt, fpar, lags, ident, wffi, wffo, out):
    ctx = ExitStack()
    with ctx:
        def sb(name, shape):
            return ctx.enter_context(nc.sbuf_tensor(name, shape, F32))

        def sem(name):
            return ctx.enter_context(nc.semaphore(name))

        bank = [ctx.enter_context(nc.psum_tensor(f"bank{i}", [128, 512], F32)) for i in range(8)]

        ident_sb = sb("ident_sb", [128, 128])
        wproj_sb = sb("wproj_sb", [128, KCH, D])
        posb_sb = sb("posb_sb", [ROWS, 2, D])
        pos_sb = sb("pos_sb", [ROWS, D])
        wlinA_sb = sb("wlinA_sb", [128, ZC])
        wlinB_sb = sb("wlinB_sb", [128, ZC])
        convw_sb = sb("convw_sb", [128, len(ZCH), 4])
        woutA_sb = sb("woutA_sb", [128, D])
        woutB_sb = sb("woutB_sb", [128, D])
        wffi_sb = sb("wffi_sb", [128, 2, NODES])
        wffo_sb = sb("wffo_sb", [128, D])
        warm_sb = sb("warm_sb", [128, 512])
        neghalf = sb("neghalf", [ROWS, BATCH])

        xbuf = sb("xbuf", [128, BATCH, KCH * ROWS])
        h = sb("h", [ROWS, TILES, D])
        u = sb("u", [ROWS, 2 * BATCH, D])
        stats = sb("stats", [ROWS, 2, 6])
        mv = sb("mv", [ROWS, TILES, 2])
        vareps = sb("vareps", [ROWS, BATCH])
        rstd = sb("rstd", [ROWS, TILES])
        uTA = sb("uTA", [128, BATCH * ROWS])
        uTB = sb("uTB", [128, BATCH * ROWS])
        zc = sb("zc", [128, 2, len(ZCH), BATCH * ROWS])
        nmax = sb("nmax", [ROWS, TILES, ORDERS])
        esum = sb("esum", [ROWS, TILES, ORDERS])
        rsum = sb("rsum", [ROWS, TILES, ORDERS])
        stage = sb("stage", [ROWS, BATCH, GROUPS, ORDERS + 1, DG])
        X3 = sb("X3", [ROWS, SLOTS, ORDERS + 1, DG])
        filt_sb = sb("filt_sb", [128, 2, ORDERS, 2 * POS])
        fpar_sb = sb("fpar_sb", [128, 2, 4])
        lags_sb = sb("lags_sb", [128, POS])
        env = sb("env", [128, 2, POS])
        fabs = sb("fabs", [128, 2, ORDERS, POS])
        rnorm = sb("rnorm", [128, ORDERS, POS])
        ones_sb = sb("ones_sb", [128, 128])
        scratch = nc.dram_tensor("filter_rows", [2 * 128, ORDERS, COPIES * 2 * POS], F32, kind="Internal").ap()
        toep = [sb(f"toep{i}", [ROWS, DG, ROWS]) for i in range(ORDERS)]
        xflat = xbuf[:, :, :].rearrange("p a b -> p (a b)")
        zflat = zc[:, 0].rearrange("p a b -> p (a b)")
        ytmp = [zflat[0:ROWS, k * 512:(k + 1) * 512].rearrange("p (a b) -> p a b", a=BLK) for k in range(2)]
        vTA = [xflat[:, k * ROWS:(k + 1) * ROWS] for k in range(2)]
        vTB = [xflat[:, (2 + k) * ROWS:(3 + k) * ROWS] for k in range(2)]
        n2TA, n2TB = uTA, uTB
        tflat = toep[0][:, :, :].rearrange("p a b -> p (a b)")
        used = [0]

        def part(n):
            used[0] += n
            return tflat[:, used[0] - n:used[0]]

        act_ = [part(len(ts) * NODES).rearrange("p (t n) -> p t n", n=NODES) for ts in HALVES]
        sgn = [part(len(ts) * 15).rearrange("p (t n) -> p t n", n=15) for ts in HALVES]
        reach = [part(len(ts) * (TREE + 1)).rearrange("p (t n) -> p t n", n=TREE + 1) for ts in HALVES]
        coef = [part(len(ts) * (TREE + 1)).rearrange("p (t n) -> p t n", n=TREE + 1) for ts in HALVES]
        q = [part(len(ts) * 8).rearrange("p (t n) -> p t n", n=8) for ts in HALVES]
        last = [part(len(ts) * 6).rearrange("p (t n) -> p t n", n=6) for ts in HALVES]
        sums = [part(len(ts) * 2).rearrange("p (t n) -> p t n", n=2) for ts in HALVES]
        coefT = sb("coefT", [128, 2, BATCH * ROWS])

        WARM_START, WARM_MOVE = 4, 12

        warm_ready = sem("warm_ready")
        w_first = sem("w_first")
        w_pos = sem("w_pos")
        w_rest = sem("w_rest")
        w_late = sem("w_late")
        w_filt = sem("w_filt")
        x_in = [sem(f"x_in{k}") for k in range(BATCH)]
        const_ready = sem("const_ready")
        ones_ready = sem("ones_ready")
        pos_ready = sem("pos_ready")
        tok_ready = sem("tok_ready")
        h_ready = sem("h_ready")
        st_ready = sem("st_ready")
        mv_ready = sem("mv_ready")
        ve_ready = sem("ve_ready")
        rstd_ready = sem("rstd_ready")
        u_ready = sem("u_ready")
        uT_ready = sem("uT_ready")
        uT_copied = sem("uT_copied")
        z_ready = sem("z_ready")
        tap2_ready = sem("tap2_ready")
        tap1_ready = sem("tap1_ready")
        zc_ready = sem("zc_ready")
        xs_ready = sem("xs_ready")
        v_ready = sem("v_ready")
        max_ready = sem("max_ready")
        exp_ready = sem("exp_ready")
        rsum_ready = sem("rsum_ready")
        gate_ready = sem("gate_ready")
        gate_last = sem("gate_last")
        vtok_ready = sem("vtok_ready")
        moved = [sem(f"moved{k}") for k in range(2)]
        env_exp = sem("env_exp")
        filt_step = sem("filt_step")
        norm_all = sem("norm_all")
        filt_saved = sem("filt_saved")
        toep_zero = sem("toep_zero")
        toep_in = [sem(f"toep_in{i}") for i in range(ORDERS)]
        y_ready = sem("y_ready")
        gated = sem("gated")
        v_added = sem("v_added")
        wout_ready = sem("wout_ready")
        vT_ready = sem("vT_ready")
        vT_copied = sem("vT_copied")
        o_ready = sem("o_ready")
        h2_ready = sem("h2_ready")
        st2_ready = sem("st2_ready")
        mv2_ready = sem("mv2_ready")
        ve2_ready = sem("ve2_ready")
        rstd2_ready = sem("rstd2_ready")
        n2_ready = sem("n2_ready")
        n2T_ready = sem("n2T_ready")
        n2T_copied = sem("n2T_copied")
        logit_ready = sem("logit_ready")
        gelu_ready = sem("gelu_ready")
        tree = sem("tree")
        coef_ready = sem("coef_ready")
        cT_ready = sem("cT_ready")
        cT_copied = sem("cT_copied")
        ffn_ready = sem("ffn_ready")
        out_ready = sem("out_ready")
        stored = sem("stored")

        BACK = {1: [0], 2: [1], 3: [2, 3]}

        def back(g, c):
            return [STEPS[g][k] for k in BACK.get(c, []) if 0 <= g and k < len(STEPS[g])]

        def at(g, k):
            return STEPS[g][k:k + 1] if 0 <= g < len(STEPS) and k >= 0 else []

        def pairs_of(g):
            return list(range(STEPS[g][0] // 2, STEPS[g][-1] // 2 + 1))

        def turned_after(g, k, n):
            if n == 2:
                return pairs_of(g) if k == 1 else []
            return pairs_of(g)[k - 2:k - 1] if k >= 2 else []

        PAIRS = [[ts[k], ts[k + 1]] for ts in STEPS for k in range(0, len(ts), 2)]
        MOVES = GROUPS * TILE_IMAGES

        def f_bank(p):
            return bank[(3, 0, 1, 4)[p % 4]]

        def cT_bank(g):
            return bank[5 if g % 2 else 7]

        def v_bank(t):
            return bank[1 if t % 2 else 7]

        def xs_bank(t):
            return bank[3 if t % 2 else 6]

        def tok_bank(t):
            return bank[t % 2 if t < 2 * BATCH else 0]

        block = ctx.enter_context(nc.Block())

        @block.sync
        def _(sp):
            sp.dma_start(wproj_sb[:, :, :], wproj).then_inc(w_first, 16)

            def load(t):
                if t >= BATCH:
                    sp.wait_ge(tok_ready, t - BATCH + 1)
                sp.dma_start(xbuf[:, t % BATCH, :], xT[t]).then_inc(x_in[t % BATCH], 16)

            load(0)
            sp.dma_start(posb_sb[:, :, :], posb).then_inc(w_pos, 16)
            for t in STEPS[0][1:]:
                load(t)
            for dst, src in ((ident_sb[:, :], ident), (wlinA_sb[:, :], wlinA), (wlinB_sb[:, :], wlinB),
                             (convw_sb[:, :, :], convw)):
                sp.dma_start(dst, src).then_inc(w_rest, 16)
            for t in STEPS[1]:
                load(t)
            for dst, src in ((woutA_sb[:, :], woutA), (woutB_sb[:, :], woutB),
                             (wffi_sb[:, :, :], wffi), (wffo_sb[:, :], wffo)):
                sp.dma_start(dst, src).then_inc(w_late, 16)

            def move(p):
                if p < len(PAIRS) - 1:
                    sp.wait_ge(gate_ready, 2 * p + 2)
                else:
                    sp.wait_ge(gate_last, 2)
                sp.wait_ge(vtok_ready, 2 * p + 2)
                t0, s0 = 2 * p, (2 * p) % BATCH
                for j in range(TILE_IMAGES):
                    for g in range(GROUPS):
                        sp.dma_start(
                            X3[g * POS:(g + 1) * POS, TILE_IMAGES * t0 + j:TILE_IMAGES * (t0 + 1) + j + 1:TILE_IMAGES]
                            .rearrange("p b a d -> p b (a d)"),
                            stage[j * POS:(j + 1) * POS, s0:s0 + 2, g].rearrange("p t a d -> p t (a d)"),
                        ).then_inc(moved[p % 2], 16)

            for p in range(len(PAIRS)):
                move(p)
            for p in range(len(PAIRS)):
                sp.wait_ge(out_ready, p + 1)
                sp.dma_start(out[:, 2 * p:2 * p + 2, :], h[:, 2 * p:2 * p + 2, :]).then_inc(stored, 16)
            sp.wait_ge(stored, 16 * len(PAIRS))

        @block.gpsimd
        def _(pool):
            for dst, src in ((filt_sb[:, :, :, :], filt), (fpar_sb[:, :, :], fpar), (lags_sb[:, :], lags)):
                pool.dma_start(dst, src).then_inc(w_filt, 16)
            nc.gpsimd.memset(neghalf[:, :], -0.5).then_inc(const_ready, 1)
            nc.gpsimd.memset(zc[:, :, :, :], 0.0).then_inc(const_ready, 1)

            nc.gpsimd.memset(ones_sb[:, :], 1.0).then_inc(const_ready, 1)
            nc.gpsimd.memset(coefT[:, :, :], 0.0).then_inc(const_ready, 1)
            nc.gpsimd.memset(toep[0][:, :, :], 0.0).then_inc(toep_zero, 1)

            def rsqrt(g, var, mv_sem, ve_sem, out_sem):
                ts = STEPS[g]
                pool.wait_ge(mv_sem, ts[-1] + 1)
                nc.gpsimd.tensor_scalar(vareps[:, 0:len(ts)], mv[:, ts[0]:ts[-1] + 1, 1], EPS, None, ALU.add).then_inc(ve_sem, 1)
                pool.wait_ge(ve_sem, g + 1)
                nc.gpsimd.tensor_tensor(rstd[:, ts[0]:ts[-1] + 1], vareps[:, 0:len(ts)], neghalf[:, 0:len(ts)],
                                        ALU.pow).then_inc(out_sem, 1)

            pool.wait_ge(const_ready, 4)
            rsqrt(0, mv, mv_ready, ve_ready, rstd_ready)
            nc.gpsimd.memset(toep[1][:, :, :], 0.0).then_inc(toep_zero, 1)
            rsqrt(1, mv, mv_ready, ve_ready, rstd_ready)

            pool.wait_ge(filt_step, 9)
            for c in range(2):
                for i in range(ORDERS):
                    pool.dma_start(
                        scratch[c * 128:(c + 1) * 128, i].rearrange("p (b l) -> p b l", b=COPIES),
                        filt_sb[:, c, i].unsqueeze(1).broadcast_to([128, COPIES, 2 * POS])).then_inc(filt_saved, 16)
            pool.wait_ge(filt_saved, 16 * 2 * ORDERS)
            pool.wait_ge(toep_zero, ORDERS)

            def shifts(i, which):
                copy, row, channel = 2 * POS, COPIES * 2 * POS, ORDERS * COPIES * 2 * POS
                for g, m0 in which:
                        src = bass.AP(scratch.tensor, g * DG * channel + i * row + POS - m0,
                                      [[copy - 1, COPIES], [channel, DG], [1, POS]])
                        pool.dma_start(toep[i][g * POS + m0:g * POS + m0 + COPIES, :, g * POS:(g + 1) * POS],
                                       src).then_inc(toep_in[i], 16)

            blocks = [(g, m0) for g in range(GROUPS) for m0 in range(0, POS, COPIES)]
            shifts(0, blocks)

            def softmax_scale(t):
                pool.wait_ge(exp_ready, 2 * t + 2)
                pool.wait_ge(rsum_ready, t + 1)
                for i in range(ORDERS):
                    s = stage[:, t % BATCH, :, i, :]
                    ins = nc.gpsimd.tensor_scalar(s, s, rsum[:, t, i:i + 1], None, ALU.mult)
                ins.then_inc(gate_ready, 1)

            for g in range(len(STEPS)):
                if g + 2 < len(STEPS):
                    rsqrt(g + 2, mv, mv_ready, ve_ready, rstd_ready)
                if g < len(STEPS) - 1:
                    for t in STEPS[g]:
                        softmax_scale(t)
                        shifts(1, blocks[t - BATCH:t - BATCH + 1] if t >= BATCH else [])
            for g in range(len(STEPS)):
                rsqrt(g, mv, mv2_ready, ve2_ready, rstd2_ready)

        @block.scalar
        def _(act):
            def evac_T(src, pair, ready, copied, dstA, dstB):
                act.wait_ge(ready, pair + 1)
                c = (2 * pair % BATCH) * ROWS
                nc.scalar.copy(dstA[:, c:c + 2 * ROWS], src[0:128, 0:2 * ROWS]).then_inc(copied, 1)
                nc.scalar.copy(dstB[0:64, c:c + 2 * ROWS], src[0:64, 2 * ROWS:4 * ROWS]).then_inc(copied, 1)

            act.wait_ge(w_filt, 16 * 3)
            for c in range(2):
                nc.scalar.activation(env[:, c], lags_sb[:, :], ACT.Exp, scale=fpar_sb[:, c, 0:1]).then_inc(env_exp, 1)
            act.wait_ge(w_rest, 16 * 4)
            act.wait_ge(const_ready, 4)
            def last_tap(g, c):
                n = len(ZCH) * g + c
                m, imgs = ZCH[c][1], len(STEPS[g]) * TILE_IMAGES
                act.wait_ge(z_ready, n + 1)
                if g >= 2 and c == 0:
                    act.wait_ge(v_ready, STEPS[g - 1][0])
                dst = zc[0:m, g % 2, c, 0:imgs * POS].rearrange("p (b l) -> p b l", l=POS)[:, :, 0:SEQ]
                src = bank[4 + n % 2][0:m, 0:imgs * SEQ].rearrange("p (b l) -> p b l", l=SEQ)
                nc.scalar.activation(dst, src, ACT.Identity, bias=convw_sb[0:m, c, 3:4],
                                     scale=convw_sb[0:m, c, 2:3]).then_inc(tap2_ready, 1)

            def exponentials(t):
                act.wait_ge(max_ready, t + 1)
                if t >= BATCH:
                    p = (t - BATCH) // 2
                    act.wait_ge(moved[p % 2], 16 * MOVES * (p // 2 + 1))
                for i in range(ORDERS):
                    nc.scalar.activation(
                        stage[:, t % BATCH, :, i, :],
                        xs_bank(t)[0:ROWS, i * D:(i + 1) * D].rearrange("p (g d) -> p g d", g=GROUPS),
                        ACT.Exp, bias=nmax[:, t, i:i + 1], accum_out=esum[:, t, i:i + 1]).then_inc(exp_ready, 1)

            def u_evac(g):
                for p in range(STEPS[g][0] // 2, STEPS[g][-1] // 2 + 1):
                    evac_T(bank[2], p, uT_ready, uT_copied, uTA, uTB)

            def load(t):
                act.wait_ge(tok_ready, t - BATCH + 1)
                act.dma_start(xbuf[:, t % BATCH, :], xT[t]).then_inc(x_in[t % BATCH], 16)

            for t in STEPS[2]:
                load(t)
            u_evac(0)
            for g in range(len(STEPS) + 1):
                for c in range(len(ZCH)):
                    if g < len(STEPS):
                        last_tap(g, c)
                    for t in back(g - 1, c):
                        exponentials(t)
                    for t in at(g + 3, c - 1) if 1 <= c <= 3 else []:
                        load(t)
                if g + 1 < len(STEPS):
                    u_evac(g + 1)
                for t in at(g + 3, 3):
                    load(t)

            def vT_evac(t):
                act.wait_ge(vT_ready, t + 1)
                if t >= 2:
                    act.wait_ge(o_ready, t - 1)
                src = bank[t % 2][0:64, 0:3 * ROWS].rearrange("p (j g l) -> p g j l", g=GROUPS, j=TILE_IMAGES)
                for g, dst in enumerate((vTA[t % 2][0:64], vTA[t % 2][64:128], vTB[t % 2][0:64])):
                    nc.scalar.copy(dst.rearrange("p (j l) -> p j l", j=TILE_IMAGES), src[:, g]).then_inc(vT_copied, 1)

            def n2_evac(p):
                evac_T(bank[2], p, n2T_ready, n2T_copied, n2TA, n2TB)

            def gelu(k):
                act.wait_ge(logit_ready, k + 1)
                n = len(HALVES[k])
                nc.scalar.activation(act_[k], bank[3 if k == 0 else 6][0:ROWS, 0:n * NODES].rearrange("p (t n) -> p t n", n=NODES),
                                     ACT.Gelu).then_inc(gelu_ready, 1)

            def c_evac(g):
                act.wait_ge(cT_ready, g + 1)
                if g >= 2:
                    act.wait_ge(ffn_ready, 2 * (g - 1))
                n = len(STEPS[g]) * ROWS
                nc.scalar.copy(coefT[0:NODES, g % 2, 0:n], cT_bank(g)[0:NODES, 0:n]).then_inc(cT_copied, 1)

            for g, ts in enumerate(STEPS):
                if g == LATE + 1:
                    gelu(0)
                for k, t in enumerate(ts):
                    vT_evac(t)
                    if g:
                        for p in turned_after(g - 1, k, len(ts)):
                            n2_evac(p)
            for p in pairs_of(len(STEPS) - 1):
                n2_evac(p)
            gelu(1)
            for g in range(len(STEPS)):
                c_evac(g)

        @block.vector
        def _(dve):
            def tt(o, a, b, op):
                return nc.vector.tensor_tensor(o, a, b, op)

            nc.vector.memset(warm_sb[:, :], 0.0).then_inc(warm_ready, 1)
            nc.vector.memset(uTB[64:128, :], 0.0).then_inc(ones_ready, 1)
            dve.wait_ge(ones_ready, 1)
            nc.vector.memset(uTB[64:65, :], 1.0).then_inc(ones_ready, 1)
            dve.wait_ge(w_pos, 16)
            tt(pos_sb[:, :], posb_sb[:, 0], posb_sb[:, 1], ALU.add).then_inc(pos_ready, 1)
            dve.wait_ge(pos_ready, 1)

            def moments(t, h_sem, st_sem, mv_sem):
                dve.wait_ge(h_sem, t + 1)
                nc.vector.bn_stats(stats[:, t % 2], h[:, t]).then_inc(st_sem, 1)
                dve.wait_ge(st_sem, t + 1)
                nc.vector.bn_aggr(mv[:, t], stats[:, t % 2]).then_inc(mv_sem, 1)

            def embed(t):
                dve.wait_ge(tok_ready, t + 1)
                tt(h[:, t], tok_bank(t)[0:ROWS, 0:D], pos_sb[:, :], ALU.add).then_inc(h_ready, 1)
                moments(t, h_ready, st_ready, mv_ready)

            def normalise(ts, rstd_sem, out_sem):
                for t in ts:
                    dve.wait_ge(rstd_sem, t // BATCH + 1)
                    nc.vector.tensor_scalar(u[:, t % (2 * BATCH)], h[:, t], mv[:, t, 0:1], rstd[:, t:t + 1],
                                            ALU.subtract, ALU.mult).then_inc(out_sem, 1)

            def first_taps(g, c):
                n = len(ZCH) * g + c
                m, imgs = ZCH[c][1], len(STEPS[g]) * TILE_IMAGES
                dst = zc[0:m, g % 2, c, 0:imgs * POS].rearrange("p (b l) -> p b l", l=POS)
                src = bank[4 + n % 2][0:m, 0:imgs * SEQ].rearrange("p (b l) -> p b l", l=SEQ)
                dve.wait_ge(tap2_ready, n + 1)
                nc.vector.scalar_tensor_tensor(dst[:, :, 1:SEQ], src[:, :, 0:SEQ - 1], convw_sb[0:m, c, 1:2],
                                               dst[:, :, 1:SEQ], ALU.mult, ALU.add).then_inc(tap1_ready, 1)
                dve.wait_ge(tap1_ready, n + 1)
                nc.vector.scalar_tensor_tensor(dst[:, :, 2:SEQ], src[:, :, 0:SEQ - 2], convw_sb[0:m, c, 0:1],
                                               dst[:, :, 2:SEQ], ALU.mult, ALU.add).then_inc(zc_ready, 1)

            def maxima_and_v(t):
                dve.wait_ge(xs_ready, t + 1)
                nc.vector.tensor_reduce(nmax[:, t, :], xs_bank(t)[0:ROWS, 0:2 * D].rearrange("p (a d) -> p a d", a=2),
                                        AX_X, ALU.max, negate=True).then_inc(max_ready, 1)
                dve.wait_ge(v_ready, t + 1)
                if t >= BATCH:
                    p = (t - BATCH) // 2
                    dve.wait_ge(moved[p % 2], 16 * MOVES * (p // 2 + 1))
                tt(stage[:, t % BATCH, :, ORDERS, :], v_bank(t)[0:ROWS, 0:D].rearrange("p (g d) -> p g d", g=GROUPS),
                   u[:, t % (2 * BATCH)].rearrange("p (g d) -> p g d", g=GROUPS), ALU.add).then_inc(vtok_ready, 1)

            def inverse_sums(t):
                dve.wait_ge(exp_ready, 2 * t + 2)
                nc.vector.reciprocal(rsum[:, t, :], esum[:, t, :]).then_inc(rsum_ready, 1)

            f = filt_sb[:, :, :, POS:POS + SEQ]
            done = [0]

            def step(*made):
                for ins in made:
                    ins.then_inc(filt_step, 1)
                    done[0] += 1
                dve.wait_ge(filt_step, done[0])

            def filters_windowed():
                fa = fabs[:, :, :, 0:SEQ]
                dve.wait_ge(w_filt, 16 * 3)
                dve.wait_ge(env_exp, 2)
                step(*(nc.vector.scalar_tensor_tensor(
                    f[:, c], env[:, c, 0:SEQ].unsqueeze(1).broadcast_to([128, ORDERS, SEQ]), fpar_sb[:, c, 1:2],
                    f[:, c], ALU.add, ALU.mult) for c in range(2)))
                step(nc.vector.tensor_scalar(fa.rearrange("p c i l -> p (c i) l"), f.rearrange("p c i l -> p (c i) l"), -1.0, None, ALU.mult))
                step(tt(fa.rearrange("p c i l -> p (c i) l"), fa.rearrange("p c i l -> p (c i) l"),
                        f.rearrange("p c i l -> p (c i) l"), ALU.max))

            def filters_normed():
                dve.wait_ge(norm_all, 1)
                sums_ = bank[3][0:128, 0:ORDERS * SEQ].rearrange("p (i l) -> p i l", i=ORDERS)
                step(nc.vector.reciprocal(rnorm[:, :, 0:SEQ], sums_))
                step(*(tt(f[:, c], f[:, c], rnorm[:, :, 0:SEQ], ALU.mult) for c in range(2)))
                step(*(tt(f[:, c, :, 0:1], f[:, c, :, 0:1], fpar_sb[:, c, 2:4].unsqueeze(2), ALU.add) for c in range(2)))

            for t in STEPS[0]:
                embed(t)
            filters_windowed()
            normalise(STEPS[0], rstd_ready, u_ready)
            for t in STEPS[1][:2]:
                embed(t)
            filters_normed()
            for t in STEPS[1][2:]:
                embed(t)
            for g in range(len(STEPS) + 1):
                for c in range(len(ZCH)):
                    if g < len(STEPS):
                        first_taps(g, c)
                    for t in back(g - 1, c - 1):
                        inverse_sums(t)
                        if g == len(STEPS):
                            dve.wait_ge(rsum_ready, t + 1)
                            for i in range(ORDERS):
                                e = stage[:, t % BATCH, :, i, :]
                                ins = nc.vector.tensor_scalar(e, e, rsum[:, t, i:i + 1], None, ALU.mult)
                            ins.then_inc(gate_last, 1)
                    for t in back(g - 1, c):
                        maxima_and_v(t)
                    for k in BACK.get(c, []):
                        for t in at(g + 1, k):
                            if t >= 2 * BATCH:
                                dve.wait_ge(vtok_ready, t - 2 * BATCH + 1)
                            normalise([t], rstd_ready, u_ready)
                    for t in at(g + 2, c) if c < 3 else []:
                        embed(t)
                for t in at(g + 2, 3):
                    embed(t)

            dve.wait_ge(w_late, 16 * 4)
            tt(woutA_sb[:, 0:128], woutA_sb[:, 0:128], ident_sb[:, :], ALU.add).then_inc(wout_ready, 1)
            tt(woutB_sb[0:64, 128:D], woutB_sb[0:64, 128:D], ident_sb[0:64, 0:64], ALU.add).then_inc(wout_ready, 1)
            for k in range(2):
                nc.vector.memset(vTB[k][64:128, :], 0.0).then_inc(wout_ready, 1)
            dve.wait_ge(wout_ready, 4)
            for k in range(2):
                nc.vector.memset(vTB[k][64:65, :], 1.0).then_inc(wout_ready, 1)

            n = 0
            for i in range(ORDERS):
                for k in range(NBLK):
                    dve.wait_ge(y_ready, n + 1)
                    gate = X3[:, 0:IMAGES, i, k * BLK:(k + 1) * BLK].rearrange("p b d -> p d b")
                    v = X3[:, 0:IMAGES, ORDERS, k * BLK:(k + 1) * BLK].rearrange("p b d -> p d b")
                    y = bank[[0, 1, 4, 5][n % 4]][0:ROWS, :].rearrange("p (d b) -> p d b", d=BLK)
                    tt(ytmp[n % 2], y, gate, ALU.mult).then_inc(gated, 1)
                    dve.wait_ge(gated, n + 1)
                    tt(v, v, ytmp[n % 2], ALU.add).then_inc(v_added, 1)
                    n += 1

            def residual(ts):
                for t in ts:
                    dve.wait_ge(o_ready, t + 1)
                    tt(h[:, t], bank[4 + t % 2][0:ROWS, 0:D], h[:, t], ALU.add).then_inc(h2_ready, 1)
                    moments(t, h2_ready, st2_ready, mv2_ready)

            steps = [0]

            def link(ins):
                ins.then_inc(tree, 1)
                steps[0] += 1
                dve.wait_ge(tree, steps[0])

            def walk(k):
                ts = HALVES[k]
                a, s, r, c, qq = act_[k], sgn[k], reach[k], coef[k], q[k]
                dve.wait_ge(gelu_ready, k + 1)
                logits = bank[3 if k == 0 else 6][0:ROWS, 0:len(ts) * NODES].rearrange("p (t n) -> p t n", n=NODES)
                link(nc.vector.tensor_scalar(s, logits[:, :, 0:15], 0.0, None, ALU.is_gt))
                nc.vector.tensor_copy(r[:, :, 2:3], s[:, :, 0:1])
                nc.vector.tensor_scalar(r[:, :, 1:2], s[:, :, 0:1], -1.0, 1.0, ALU.mult, ALU.add)
                link(tt(c[:, :, 2:3], a[:, :, 0:1], s[:, :, 0:1], ALU.mult))
                link(tt(c[:, :, 1:2], a[:, :, 0:1], c[:, :, 2:3], ALU.subtract))
                for lo, hi in ((1, 3), (3, 7), (7, 15)):
                    w = hi - lo
                    right = slice(2 * lo + 2, 2 * hi + 1, 2)
                    left = slice(2 * lo + 1, 2 * hi, 2)
                    tt(r[:, :, right], r[:, :, lo:hi], s[:, :, lo:hi], ALU.mult)
                    link(tt(qq[:, :, 0:w], r[:, :, lo:hi], a[:, :, lo:hi], ALU.mult))
                    tt(r[:, :, left], r[:, :, lo:hi], r[:, :, right], ALU.subtract)
                    link(tt(c[:, :, right], qq[:, :, 0:w], s[:, :, lo:hi], ALU.mult))
                    link(tt(c[:, :, left], qq[:, :, 0:w], c[:, :, right], ALU.subtract))
                nl = NODES - 1
                nc.vector.tensor_reduce(sums[k][:, :, 0:1], c[:, :, nl:TREE], AX_X, ALU.add)
                link(nc.vector.tensor_reduce(sums[k][:, :, 1:2], r[:, :, nl:TREE], AX_X, ALU.add))
                link(nc.vector.tensor_copy(r[:, :, nl:nl + 1], sums[k][:, :, 1:2]))
                link(tt(last[k], r[:, :, 15:NODES], a[:, :, 15:NODES], ALU.mult))
                link(nc.vector.tensor_reduce(sums[k][:, :, 1:2], last[k], AX_X, ALU.add))
                link(tt(sums[k][:, :, 0:1], sums[k][:, :, 0:1], sums[k][:, :, 1:2], ALU.add))
                link(nc.vector.scalar_tensor_tensor(c[:, :, nl:nl + 1], a[:, :, nl:nl + 1], 5.0,
                                                    sums[k][:, :, 0:1], ALU.mult, ALU.add))
                nc.vector.memset(c[:, :, 0:1], 0.0).then_inc(coef_ready, 1)

            for g in range(len(STEPS)):
                residual(STEPS[g][:1])
                if g >= 1:
                    if g >= 3:
                        dve.wait_ge(n2T_ready, STEPS[g - 3][-1] // 2 + 1)
                    normalise(STEPS[g - 1], rstd2_ready, n2_ready)
                residual(STEPS[g][1:])
            normalise(STEPS[-1], rstd2_ready, n2_ready)
            walk(0)
            walk(1)
            for p in range(len(PAIRS)):
                dve.wait_ge(ffn_ready, p + 1)
                tt(h[:, 2 * p:2 * p + 2].rearrange("p t d -> p (t d)"), f_bank(p)[0:ROWS, 0:2 * D],
                   h[:, 2 * p:2 * p + 2].rearrange("p t d -> p (t d)"), ALU.add).then_inc(out_ready, 1)

        @block.tensor
        def _(pe):
            mm = nc.tensor.matmul

            def warm_up(n):
                for _ in range(n):
                    mm(bank[2][:, :], warm_sb[:, 0:128], warm_sb[:, :], start=True, stop=True)

            pe.wait_ge(warm_ready, 1)
            warm_up(WARM_START)

            def embed(t):
                pe.wait_ge(x_in[t % BATCH], 16 * (t // BATCH + 1))
                if t >= 2 * BATCH:
                    pe.wait_ge(h_ready, t)
                elif t >= 2:
                    pe.wait_ge(h_ready, t - 1)
                for c in range(KCH):
                    ins = mm(tok_bank(t)[0:ROWS, 0:D], xbuf[:, t % BATCH, c * ROWS:(c + 1) * ROWS],
                             wproj_sb[:, c, :], start=(c == 0), stop=(c == KCH - 1))
                ins.then_inc(tok_ready, 1)

            def turn(p, src_sem, ready, copied):
                pe.wait_ge(src_sem, 2 * p + 2)
                if p:
                    pe.wait_ge(copied, 2 * p)
                for k in range(2):
                    s = u[:, (2 * p + k) % (2 * BATCH), :]
                    nc.tensor.transpose(bank[2][0:128, k * ROWS:(k + 1) * ROWS], s[:, 0:128], ident_sb[0:ROWS, 0:ROWS])
                for k in range(2):
                    s = u[:, (2 * p + k) % (2 * BATCH), :]
                    ins = nc.tensor.transpose(bank[2][0:64, (2 + k) * ROWS:(3 + k) * ROWS], s[:, 128:D],
                                              ident_sb[0:ROWS, 0:ROWS])
                ins.then_inc(ready, 1)

            def in_project(g, c):
                n = len(ZCH) * g + c
                (c0, m), imgs = ZCH[c], len(STEPS[g]) * TILE_IMAGES
                pe.wait_ge(uT_copied, STEPS[g][-1] + 1)
                if n >= 2:
                    pe.wait_ge(zc_ready, n - 1)
                dst = bank[4 + n % 2][0:m, 0:imgs * SEQ].rearrange("p (b l) -> p b l", l=SEQ)
                for w, src, rows, a in ((wlinA_sb, uTA, 128, True), (wlinB_sb, uTB, 128, False)):
                    rhs = src[0:rows, 0:imgs * POS].rearrange("p (b l) -> p b l", l=POS)[:, :, 0:SEQ]
                    ins = mm(dst, w[0:rows, c0:c0 + m], rhs, start=a, stop=not a)
                ins.then_inc(z_ready, 1)

            def turn_back(t):
                g = t // BATCH
                pe.wait_ge(zc_ready, len(ZCH) * (g + 1))
                if t >= 2:
                    pe.wait_ge(exp_ready, 2 * (t - 1))
                    pe.wait_ge(vtok_ready, t - 1)
                cols = slice((t % BATCH) * ROWS, (t % BATCH + 1) * ROWS)
                for c in range(3):
                    ins = nc.tensor.transpose(xs_bank(t)[0:ROWS, c * 128:(c + 1) * 128], zc[:, g % 2, c, cols], ident_sb[:, :])
                ins.then_inc(xs_ready, 1)
                nc.tensor.transpose(v_bank(t)[0:ROWS, 0:128], zc[:, g % 2, 3, cols], ident_sb[:, :])
                nc.tensor.transpose(v_bank(t)[0:ROWS, 128:D], zc[0:64, g % 2, 4, cols],
                                    ident_sb[0:64, 0:64]).then_inc(v_ready, 1)

            pe.wait_ge(w_first, 16)
            for t in STEPS[0]:
                embed(t)
            embed(STEPS[1][0])
            pe.wait_ge(filt_step, 4)
            pe.wait_ge(const_ready, 4)
            for c in range(2):
                ins = mm(bank[3][0:128, 0:ORDERS * SEQ].rearrange("p (i l) -> p i l", i=ORDERS), ones_sb[:, :],
                         fabs[:, c, :, 0:SEQ], start=(c == 0), stop=(c == 1))
            ins.then_inc(norm_all, 1)
            for t in STEPS[1][1:]:
                embed(t)
            pe.wait_ge(w_rest, 16 * 4)
            pe.wait_ge(ones_ready, 2)
            for p in range(2):
                turn(p, u_ready, uT_ready, uT_copied)
            for g in range(len(STEPS) + 1):
                for c in range(len(ZCH)):
                    if g < len(STEPS):
                        in_project(g, c)
                    for t in back(g - 1, c):
                        turn_back(t)
                    for t in at(g + 2, c) if c < 3 else []:
                        embed(t)
                for t in at(g + 1, 0):
                    turn(t // 2, u_ready, uT_ready, uT_copied)
                for t in at(g + 2, 3):
                    embed(t)
                for t in at(g + 1, 2):
                    turn(t // 2, u_ready, uT_ready, uT_copied)

            warm_up(WARM_MOVE)
            for k in range(2):
                n_pairs = len([p for p in range(len(PAIRS)) if p % 2 == k])
                pe.wait_ge(moved[k], 16 * MOVES * n_pairs)
            n = 0
            for i in range(ORDERS):
                pe.wait_ge(toep_in[i], 16 * GROUPS * POS // COPIES)
                for k in range(NBLK):
                    if n >= 4:
                        pe.wait_ge(gated, n - 3)
                    if i:
                        pe.wait_ge(v_added, k + 1)
                    for j in range(BLK):
                        d = k * BLK + j
                        ins = mm(bank[[0, 1, 4, 5][n % 4]][0:ROWS, j * IMAGES:(j + 1) * IMAGES], toep[i][:, d, :],
                                 X3[:, 0:IMAGES, ORDERS, d], start=True, stop=True)
                    ins.then_inc(y_ready, 1)
                    n += 1

            pe.wait_ge(v_added, n)
            pe.wait_ge(wout_ready, 6)

            def v_turn(t):
                if t >= 2:
                    pe.wait_ge(vT_copied, 3 * (t - 1))
                for j in range(TILE_IMAGES):
                    ins = nc.tensor.transpose(bank[t % 2][0:64, j * ROWS:(j + 1) * ROWS],
                                              X3[:, TILE_IMAGES * t + j, ORDERS, :], ident_sb[0:ROWS, 0:ROWS])
                ins.then_inc(vT_ready, 1)

            def project(t):
                pe.wait_ge(vT_copied, 3 * (t + 1))
                if t >= 2:
                    pe.wait_ge(h2_ready, t - 1)
                mm(bank[4 + t % 2][0:ROWS, 0:D], vTA[t % 2], woutA_sb[:, :], start=True, stop=False)
                mm(bank[4 + t % 2][0:ROWS, 0:D], vTB[t % 2], woutB_sb[:, :], start=False, stop=True).then_inc(o_ready, 1)

            def logits(g):
                pe.wait_ge(n2T_copied, STEPS[g][-1] + 1)
                half = 0 if g < LATE else 1
                for t in STEPS[g]:
                    o = (t - HALVES[half][0]) * NODES
                    dst = bank[3 if half == 0 else 6][0:ROWS, o:o + NODES]
                    c = (t % BATCH) * ROWS
                    mm(dst, n2TA[:, c:c + ROWS], wffi_sb[:, 0, :], start=True, stop=False)
                    ins = mm(dst, n2TB[:, c:c + ROWS], wffi_sb[:, 1, :], start=False, stop=True)
                if g in (LATE - 1, len(STEPS) - 1):
                    ins.then_inc(logit_ready, 1)

            def c_turn(g):
                half = 0 if g < LATE else 1
                pe.wait_ge(coef_ready, half + 1)
                if g >= 2:
                    pe.wait_ge(cT_copied, g - 1)
                for k, t in enumerate(STEPS[g]):
                    ins = nc.tensor.transpose(cT_bank(g)[0:NODES, k * ROWS:(k + 1) * ROWS],
                                              coef[half][:, t - HALVES[half][0], 0:NODES], ident_sb[0:ROWS, 0:ROWS])
                ins.then_inc(cT_ready, 1)

            def tree_out(g):
                pe.wait_ge(cT_copied, g + 1)
                for k, p in enumerate(pairs_of(g)):
                    if p >= 4:
                        pe.wait_ge(out_ready, p - 3)
                    for m in range(2):
                        ins = mm(f_bank(p)[0:ROWS, m * D:(m + 1) * D],
                                 coefT[:, g % 2, (2 * k + m) * ROWS:(2 * k + m + 1) * ROWS],
                                 wffo_sb[:, :], start=True, stop=True)
                    ins.then_inc(ffn_ready, 1)

            for g, ts in enumerate(STEPS):
                for k, t in enumerate(ts):
                    v_turn(t)
                    if t:
                        project(t - 1)
                    if t == TILES - 1:
                        project(t)
                    if g:
                        for p in turned_after(g - 1, k, len(ts)):
                            turn(p, n2_ready, n2T_ready, n2T_copied)
                if g:
                    logits(g - 1)
            for p in pairs_of(len(STEPS) - 1):
                turn(p, n2_ready, n2T_ready, n2T_copied)
            logits(len(STEPS) - 1)
            c_turn(0)
            for g in range(len(STEPS)):
                if g + 1 < len(STEPS):
                    c_turn(g + 1)
                tree_out(g)


_SHAPE_OUT = [ROWS, TILES, D]


def _laid_out(i):
    a = {k: np.asarray(v) for k, v in i.items()}
    side = SIDE // PATCH
    f = np.float32
    p = a["x"].reshape(IMAGES, CHANNELS_IN, side, PATCH, side, PATCH).transpose(0, 2, 4, 1, 3, 5)
    x = np.zeros((SLOTS, POS, KDIM), f)
    x[:IMAGES, 1:SEQ] = p.reshape(IMAGES, PATCHES, KDIM)
    xT = x.reshape(TILES, ROWS, KCH, 128).transpose(0, 3, 2, 1).reshape(TILES, 128, KCH * ROWS)
    wproj = a["L0_tok_proj_w"].T.reshape(KCH, 128, D).transpose(1, 0, 2)
    posb = np.zeros((TILE_IMAGES, POS, 2, D), f)
    posb[:, :SEQ, 0] = a["L0_tok_pos_embedding"][0]
    posb[:, 0, 1] = a["L0_tok_cls_token"][0, 0]
    posb[:, 1:SEQ, 1] = a["L0_tok_proj_b"]
    wl = a["L0_attn_W_lin"].T
    wlinB = np.zeros((128, ZC), f)
    wlinB[:64], wlinB[64] = wl[128:], a["L0_attn_b_lin"]
    cw = np.zeros((len(ZCH) * 128, 4), f)
    cw[:ZC, 0:3], cw[:ZC, 3] = a["L0_attn_conv_w"][:, 0], a["L0_attn_conv_b"]
    convw = cw.reshape(len(ZCH), 128, 4).transpose(1, 0, 2)
    wo = a["L0_attn_W_out"].T
    woutB = np.zeros((128, D), f)
    woutB[:64], woutB[64] = wo[128:], a["L0_attn_b_out"]
    filt = np.zeros((2 * 128, ORDERS, 2 * POS), f)
    filt[:D, :, POS:POS + SEQ] = a["L0_attn_h_param"][:, :, :SEQ].transpose(1, 0, 2)
    fpar = np.zeros((2 * 128, 4), f)
    fpar[:D, 0], fpar[:D, 1] = a["L0_attn_alphas"].reshape(D), a["L0_attn_win_b"].reshape(D)
    fpar[:D, 2:4] = a["L0_attn_Bmat"].reshape(ORDERS, D).T
    lags = np.zeros((128, POS), f)
    lags[:, :SEQ] = (np.arange(SEQ, dtype=f) / f(MAXLEN - 1)).astype(f)
    wi = np.zeros((256, NODES), f)
    wi[:D] = a["L0_ffn_weights_in"].T
    wffi = wi.reshape(2, 128, NODES).transpose(1, 0, 2)
    return dict(xT=xT, wproj=wproj, posb=posb.reshape(ROWS, 2, D), wlinA=wl[:128], wlinB=wlinB, convw=convw,
                woutA=wo[:128], woutB=woutB,
                filt=filt.reshape(2, 128, ORDERS, 2 * POS).transpose(1, 0, 2, 3),
                fpar=fpar.reshape(2, 128, 4).transpose(1, 0, 2), lags=lags, ident=np.eye(128, dtype=f), wffi=wffi, wffo=np.concatenate([a["L0_ffn_weights_out"], np.zeros((128 - NODES, D), f)]))


def kernel(**inputs):
    import concourse.bacc as bacc
    from concourse.bass_utils import run_bass_kernel_spmd

    nc = bacc.Bacc("TRN2", target_bir_lowering=False, num_devices=1)
    arrays, args = {}, []
    for name, a in _laid_out(inputs).items():
        a = np.ascontiguousarray(a)
        arrays[f"in_{name}"] = a
        args.append(nc.dram_tensor(f"in_{name}", a.shape, F32, kind="ExternalInput").ap())
    out = nc.dram_tensor("out_rows", _SHAPE_OUT, F32, kind="ExternalOutput").ap()
    build(nc, *args, out)
    r = run_bass_kernel_spmd(nc, [arrays], core_ids=[0])
    rows = r.results[0]["out_rows"].reshape(TILE_IMAGES, POS, TILES, D).transpose(2, 0, 1, 3)
    return rows.reshape(SLOTS, POS, D)[:IMAGES, :SEQ]
```

```python
from contextlib import ExitStack

import numpy as np

import concourse.bass as bass
from concourse import mybir

F32 = mybir.dt.float32
ALU = mybir.AluOpType
ACT = mybir.ActivationFunctionType
AX_X = mybir.AxisListType.X

IMAGES = 64
CHANNELS_IN, SIDE, PATCH = 3, 96, 16
PATCHES = (SIDE // PATCH) ** 2
SEQ = PATCHES + 1
POS = 40
TILE_IMAGES = 3
ROWS = TILE_IMAGES * POS
TILES = -(-IMAGES // TILE_IMAGES)
SLOTS = TILES * TILE_IMAGES
D = 192
KDIM = CHANNELS_IN * PATCH * PATCH
KCH = KDIM // 128
GROUPS = 3
DG = D // GROUPS
ORDERS = 2
ZC = (ORDERS + 1) * D
ZCH = [(c, min(128, ZC - c)) for c in range(0, ZC, 128)]
EPS = 1e-5
MAXLEN = 512
NODES = 21
TREE = 31
BATCH = 4
USLOTS = 3 * BATCH
STEPS = [list(range(t, min(t + BATCH, TILES))) for t in range(0, TILES, BATCH)]
SPARE_STEPS = [3, 5]
COPIES = 10
BLK = 8
NBLK = DG // BLK
LATE = 3
HALVES = [sum(STEPS[:LATE], []), sum(STEPS[LATE:], [])]


def build(nc, xT, wproj, posb, wlinA, wlinB, convw, woutA, woutB, filt, fpar, lags, ident, wffi, wffo, out):
    ctx = ExitStack()
    with ctx:
        def sb(name, shape):
            return ctx.enter_context(nc.sbuf_tensor(name, shape, F32))

        def sem(name):
            return ctx.enter_context(nc.semaphore(name))

        bank = [ctx.enter_context(nc.psum_tensor(f"bank{i}", [128, 512], F32)) for i in range(8)]

        ident_sb = sb("ident_sb", [128, 128])
        wproj_sb = sb("wproj_sb", [128, KCH, D])
        pos_sb = sb("pos_sb", [ROWS, D])
        wlinA_sb = sb("wlinA_sb", [128, ZC])
        wlinB_sb = sb("wlinB_sb", [128, ZC])
        convw_sb = sb("convw_sb", [128, len(ZCH), 4])
        woutA_sb = sb("woutA_sb", [128, D])
        woutB_sb = sb("woutB_sb", [128, D])
        wffi_sb = sb("wffi_sb", [128, 2, NODES])
        wffo_sb = sb("wffo_sb", [128, D])
        neghalf = sb("neghalf", [ROWS, BATCH])

        xbuf = sb("xbuf", [128, BATCH, KCH * ROWS])
        h = sb("h", [ROWS, TILES, D])
        u = sb("u", [ROWS, USLOTS, D])
        stats = sb("stats", [ROWS, 2, 6])
        mv = sb("mv", [ROWS, TILES, 2])
        vareps = sb("vareps", [ROWS, BATCH])
        rstd = sb("rstd", [ROWS, TILES])
        uTA = sb("uTA", [128, 2, BATCH * ROWS])
        uTB = sb("uTB", [128, 2, BATCH * ROWS])
        zc = sb("zc", [128, 2, len(ZCH), BATCH * ROWS])
        nmax = sb("nmax", [ROWS, TILES, ORDERS])
        esum = sb("esum", [ROWS, TILES, ORDERS])
        rsum = sb("rsum", [ROWS, TILES, ORDERS])
        stage = sb("stage", [ROWS, BATCH, GROUPS, ORDERS + 1, DG])
        posb_sb = stage[:, 0].rearrange("p g a d -> p (g a d)")[:, 0:2 * D].rearrange("p (a d) -> p a d", a=2)
        X3 = sb("X3", [ROWS, SLOTS, ORDERS + 1, DG])
        filt_sb = sb("filt_sb", [128, 2, ORDERS, 2 * POS])
        fpar_sb = sb("fpar_sb", [128, 2, 4])
        lags_sb = sb("lags_sb", [128, POS])
        env = sb("env", [128, 2, POS])
        fabs = sb("fabs", [128, 2, ORDERS, POS])
        rnorm = sb("rnorm", [128, ORDERS, POS])
        ones_sb = sb("ones_sb", [128, 128])
        scratch = nc.dram_tensor("filter_rows", [2 * 128, ORDERS, COPIES * 2 * POS], F32, kind="Internal").ap()
        toep = [sb(f"toep{i}", [ROWS, DG, ROWS]) for i in range(ORDERS)]
        xflat = xbuf[:, :, :].rearrange("p a b -> p (a b)")
        zflat = zc[:, 0].rearrange("p a b -> p (a b)")
        ytmp = [zflat[0:ROWS, k * 512:(k + 1) * 512].rearrange("p (a b) -> p a b", a=BLK) for k in range(2)]
        spare = xflat[0:ROWS, 4 * ROWS:4 * ROWS + BATCH * (ORDERS + 1) * D].rearrange(
            "p (t g a d) -> p t g a d", t=BATCH, g=GROUPS, a=ORDERS + 1)
        vTA = [xflat[:, k * ROWS:(k + 1) * ROWS] for k in range(2)]
        vTB = [xflat[:, (2 + k) * ROWS:(3 + k) * ROWS] for k in range(2)]
        n2TA, n2TB = uTA, uTB
        tflat = toep[0][:, :, :].rearrange("p a b -> p (a b)")
        used = [0]

        def part(n):
            used[0] += n
            return tflat[:, used[0] - n:used[0]]

        act_ = [part(len(ts) * NODES).rearrange("p (t n) -> p t n", n=NODES) for ts in HALVES]
        sgn = [part(len(ts) * 15).rearrange("p (t n) -> p t n", n=15) for ts in HALVES]
        reach = [part(len(ts) * (TREE + 1)).rearrange("p (t n) -> p t n", n=TREE + 1) for ts in HALVES]
        coef = [part(len(ts) * (TREE + 1)).rearrange("p (t n) -> p t n", n=TREE + 1) for ts in HALVES]
        q = [part(len(ts) * 8).rearrange("p (t n) -> p t n", n=8) for ts in HALVES]
        last = [part(len(ts) * 6).rearrange("p (t n) -> p t n", n=6) for ts in HALVES]
        sums = [part(len(ts) * 2).rearrange("p (t n) -> p t n", n=2) for ts in HALVES]
        coefT = sb("coefT", [128, 2, BATCH * ROWS])
        warm = coefT[:, :, :].rearrange("p a b -> p (a b)")

        WARM_START, WARM_MOVE = 2, (3, 3, 4, 2)

        warm_ready = sem("warm_ready")
        w_first = [sem(f"w_first{k}") for k in range(2)]
        w_pos = sem("w_pos")
        w_rest = sem("w_rest")
        w_late = sem("w_late")
        w_filt = sem("w_filt")
        x_in = [sem(f"x_in{k}") for k in range(BATCH)]
        const_ready = sem("const_ready")
        ones_ready = sem("ones_ready")
        pos_ready = sem("pos_ready")
        tok_ready = sem("tok_ready")
        h_ready = sem("h_ready")
        st_ready = sem("st_ready")
        mv_ready = sem("mv_ready")
        ve_ready = sem("ve_ready")
        rstd_ready = sem("rstd_ready")
        u_ready = sem("u_ready")
        uT_ready = sem("uT_ready")
        uT_copied = sem("uT_copied")
        z_ready = sem("z_ready")
        tap2_ready = sem("tap2_ready")
        tap1_ready = sem("tap1_ready")
        zc_ready = sem("zc_ready")
        xs_ready = sem("xs_ready")
        v_ready = sem("v_ready")
        max_ready = sem("max_ready")
        exp_ready = sem("exp_ready")
        rsum_ready = sem("rsum_ready")
        gate_ready = sem("gate_ready")
        gate_last = sem("gate_last")
        vtok_ready = sem("vtok_ready")
        moved = [sem(f"moved{k}") for k in range(4)]
        moved_pool = sem("moved_pool")
        env_exp = sem("env_exp")
        filt_step = sem("filt_step")
        norm_all = sem("norm_all")
        filt_saved = sem("filt_saved")
        toep_zero = sem("toep_zero")
        toep_in = [sem(f"toep_in{i}") for i in range(ORDERS)]
        y_ready = sem("y_ready")
        gated = sem("gated")
        v_added = sem("v_added")
        wout_ready = sem("wout_ready")
        vT_ready = sem("vT_ready")
        vT_copied = sem("vT_copied")
        o_ready = sem("o_ready")
        h2_ready = sem("h2_ready")
        st2_ready = sem("st2_ready")
        mv2_ready = sem("mv2_ready")
        ve2_ready = sem("ve2_ready")
        rstd2_ready = sem("rstd2_ready")
        n2_ready = sem("n2_ready")
        n2T_ready = sem("n2T_ready")
        n2T_copied = sem("n2T_copied")
        logit_ready = sem("logit_ready")
        gelu_ready = sem("gelu_ready")
        tree = sem("tree")
        coef_ready = sem("coef_ready")
        cT_ready = sem("cT_ready")
        cT_copied = sem("cT_copied")
        ffn_ready = sem("ffn_ready")
        f_copied = sem("f_copied")
        out_early = sem("out_early")
        out_ready = sem("out_ready")
        stored = sem("stored")

        BACK = {1: [0], 2: [1], 3: [2, 3]}

        def back(g, c):
            return [STEPS[g][k] for k in BACK.get(c, []) if 0 <= g and k < len(STEPS[g])]

        def at(g, k):
            return STEPS[g][k:k + 1] if 0 <= g < len(STEPS) and k >= 0 else []

        def pairs_of(g):
            return list(range(STEPS[g][0] // 2, STEPS[g][-1] // 2 + 1))

        def turned_in(g, c):
            return pairs_of(g)[c - 2:c - 1] if g < len(STEPS) and c >= 2 else []

        def turned_behind(t):
            p = (t - BATCH - 3) // BATCH * 2 + (t - BATCH - 3) % BATCH
            return [p] if t >= BATCH + 3 and (t - BATCH - 3) % BATCH < 2 else []

        def logits_behind(t):
            return [t // BATCH - 2] if t >= 2 * BATCH and t % BATCH == 1 else []

        PAIRS = [[ts[k], ts[k + 1]] for ts in STEPS for k in range(0, len(ts), 2)]

        def staged(t):
            return (spare if t // BATCH in SPARE_STEPS else stage)[:, t % BATCH:]

        def slot_free(queue, t):
            step = t // BATCH
            if step == SPARE_STEPS[0]:
                queue.wait_ge(tok_ready, TILES)
            elif step:
                p = (t - BATCH * (2 if step > SPARE_STEPS[0] else 1)) // 2
                queue.wait_ge(moved[p % 4], 16 * len(PARTS) * (p // 4 + 1))

        blocks = [(g, m0) for g in range(GROUPS) for m0 in range(0, POS, COPIES)]

        def shifts(queue, i, which):
            channel = ORDERS * COPIES * 2 * POS
            for g, m0 in which:
                src = bass.AP(scratch.tensor, g * DG * channel + i * COPIES * 2 * POS + POS - m0,
                              [[2 * POS - 1, COPIES], [channel, DG], [1, POS]])
                queue.dma_start(toep[i][g * POS + m0:g * POS + m0 + COPIES, :, g * POS:(g + 1) * POS],
                                src).then_inc(toep_in[i], 16)

        EARLY = LATE * BATCH // 2
        f_sb = [toep[1][:, :, :].rearrange("p a b -> p (a b)")[:, k * 2 * D:(k + 1) * 2 * D] for k in range(EARLY)]

        def f_rows(p):
            return h[:, 2 * p:2 * p + 2].rearrange("p t d -> p (t d)")

        def added(queue, p):
            if p < EARLY:
                queue.wait_ge(out_early, p + 1)
            else:
                queue.wait_ge(out_ready, p - EARLY + 1)

        PARTS = [(j, g) for j in range(TILE_IMAGES) for g in range(GROUPS)]
        POOL_PARTS = {len(PAIRS) - 3: 3, len(PAIRS) - 2: 3, len(PAIRS) - 1: 4}
        DVE_SCALES = STEPS[-2][0]

        def move(queue, p, parts, signal):
            if 2 * p < DVE_SCALES:
                queue.wait_ge(gate_ready, 2 * p + 2)
            else:
                queue.wait_ge(gate_last, 2 * p + 2 - DVE_SCALES)
            queue.wait_ge(vtok_ready, 2 * p + 2)
            t0 = 2 * p
            for j, g in parts:
                queue.dma_start(
                    X3[g * POS:(g + 1) * POS, TILE_IMAGES * t0 + j:TILE_IMAGES * (t0 + 1) + j + 1:TILE_IMAGES]
                    .rearrange("p b a d -> p b (a d)"),
                    staged(t0)[j * POS:(j + 1) * POS, 0:2, g].rearrange("p t a d -> p t (a d)"),
                ).then_inc(signal, 16)

        def f_bank(p):
            return bank[(3, 0, 1, 4)[p % 4]]

        def cT_bank(g):
            return bank[5 if g % 2 else 7]

        THREE = len(ZCH) * (len(STEPS) - 2)

        def z_bank(n):
            return bank[4 + n % 2] if n < THREE else bank[(0, 4, 5)[(n - THREE) % 3]]

        def v_bank(t):
            return bank[1 if t % 2 else 7]

        def xs_bank(t):
            return bank[3 if t % 2 else 6]

        def tok_bank(t):
            return bank[t % 2 if t < 2 * BATCH else 0]

        block = ctx.enter_context(nc.Block())

        @block.sync
        def _(sp):
            sp.dma_start(wproj_sb[:, 0:KCH // 2, :], wproj[:, 0:KCH // 2]).then_inc(w_first[0], 16)

            def load(t):
                if t >= BATCH:
                    sp.wait_ge(tok_ready, t - BATCH + 1)
                sp.dma_start(xbuf[:, t % BATCH, :], xT[t]).then_inc(x_in[t % BATCH], 16)

            load(0)
            sp.dma_start(wproj_sb[:, KCH // 2:, :], wproj[:, KCH // 2:]).then_inc(w_first[1], 16)
            sp.dma_start(posb_sb, posb).then_inc(w_pos, 16)
            for t in STEPS[0][1:]:
                load(t)
            for dst, src in ((ident_sb[:, :], ident), (wlinA_sb[:, :], wlinA), (wlinB_sb[:, :], wlinB),
                             (convw_sb[:, :, :], convw)):
                sp.dma_start(dst, src).then_inc(w_rest, 16)
            for t in STEPS[1]:
                load(t)
            for dst, src in ((woutA_sb[:, :], woutA), (woutB_sb[:, :], woutB),
                             (wffi_sb[:, :, :], wffi), (wffo_sb[:, :], wffo)):
                sp.dma_start(dst, src).then_inc(w_late, 16)

            sp.wait_ge(filt_saved, 16 * 2 * ORDERS)
            sp.wait_ge(toep_zero, ORDERS)
            shifts(sp, 1, blocks)
            for p in range(len(PAIRS)):
                move(sp, p, PARTS[:len(PARTS) - POOL_PARTS.get(p, 0)], moved[p % 4])
            for p in range(len(PAIRS)):
                added(sp, p)
                sp.dma_start(out[:, 2 * p:2 * p + 2, :], h[:, 2 * p:2 * p + 2, :]).then_inc(stored, 16)
            sp.wait_ge(stored, 16 * len(PAIRS))

        @block.gpsimd
        def _(pool):
            for dst, src in ((filt_sb[:, :, :, :], filt), (fpar_sb[:, :, :], fpar), (lags_sb[:, :], lags)):
                pool.dma_start(dst, src).then_inc(w_filt, 16)
            nc.gpsimd.memset(neghalf[:, :], -0.5).then_inc(const_ready, 1)
            nc.gpsimd.memset(zc[:, :, :, :], 0.0).then_inc(const_ready, 1)

            nc.gpsimd.memset(ones_sb[:, :], 1.0).then_inc(const_ready, 1)
            nc.gpsimd.memset(toep[0][:, :, :], 0.0).then_inc(toep_zero, 1)

            def rsqrt(g, mv_sem, ve_sem, out_sem):
                ts = STEPS[g]
                pool.wait_ge(mv_sem, ts[-1] + 1)
                nc.gpsimd.tensor_scalar(vareps[:, 0:len(ts)], mv[:, ts[0]:ts[-1] + 1, 1], EPS, None,
                                        ALU.add).then_inc(ve_sem, 1)
                pool.wait_ge(ve_sem, g + 1)
                nc.gpsimd.tensor_tensor(rstd[:, ts[0]:ts[-1] + 1], vareps[:, 0:len(ts)], neghalf[:, 0:len(ts)],
                                        ALU.pow).then_inc(out_sem, 1)

            pool.wait_ge(const_ready, 3)
            rsqrt(0, mv_ready, ve_ready, rstd_ready)
            nc.gpsimd.memset(toep[1][:, :, :], 0.0).then_inc(toep_zero, 1)
            rsqrt(1, mv_ready, ve_ready, rstd_ready)

            pool.wait_ge(filt_step, 9)
            for c in range(2):
                for i in range(ORDERS):
                    pool.dma_start(
                        scratch[c * 128:(c + 1) * 128, i].rearrange("p (b l) -> p b l", b=COPIES),
                        filt_sb[:, c, i].unsqueeze(1).broadcast_to([128, COPIES, 2 * POS])).then_inc(filt_saved, 16)
            pool.wait_ge(filt_saved, 16 * 2 * ORDERS)
            pool.wait_ge(toep_zero, ORDERS)

            shifts(pool, 0, blocks[:6])
            rsqrt(2, mv_ready, ve_ready, rstd_ready)
            shifts(pool, 0, blocks[6:])

            def softmax_scale(t):
                pool.wait_ge(exp_ready, 2 * t + 2)
                pool.wait_ge(rsum_ready, t + 1)
                for i in range(ORDERS):
                    s = staged(t)[:, 0, :, i, :]
                    ins = nc.gpsimd.tensor_scalar(s, s, rsum[:, t, i:i + 1], None, ALU.mult)
                ins.then_inc(gate_ready, 1)

            for g in range(len(STEPS)):
                if STEPS[g][0] < DVE_SCALES:
                    for t in STEPS[g]:
                        if g + 3 < len(STEPS) and t == STEPS[g][len(STEPS[g + 3]) - 1]:
                            rsqrt(g + 3, mv_ready, ve_ready, rstd_ready)
                        softmax_scale(t)
            for p, n in POOL_PARTS.items():
                move(pool, p, PARTS[len(PARTS) - n:], moved_pool)
            for g in range(len(STEPS)):
                rsqrt(g, mv2_ready, ve2_ready, rstd2_ready)
            for p in range(EARLY):
                pool.wait_ge(f_copied, p + 1)
                nc.gpsimd.tensor_tensor(f_rows(p), f_rows(p), f_sb[p], ALU.add).then_inc(out_early, 1)

        @block.scalar
        def _(act):
            def evac_T(src, pair, ready, copied, dstA, dstB):
                act.wait_ge(ready, pair + 1)
                half, c = 2 * pair // BATCH % 2, (2 * pair % BATCH) * ROWS
                nc.scalar.copy(dstA[:, half, c:c + 2 * ROWS], src[0:128, 0:2 * ROWS]).then_inc(copied, 1)
                nc.scalar.copy(dstB[0:64, half, c:c + 2 * ROWS], src[0:64, 2 * ROWS:4 * ROWS]).then_inc(copied, 1)

            act.wait_ge(w_filt, 16 * 3)
            for c in range(2):
                nc.scalar.activation(env[:, c], lags_sb[:, :], ACT.Exp, scale=fpar_sb[:, c, 0:1]).then_inc(env_exp, 1)
            act.wait_ge(w_rest, 16 * 4)
            act.wait_ge(const_ready, 3)
            def last_tap(g, c):
                n = len(ZCH) * g + c
                m, imgs = ZCH[c][1], len(STEPS[g]) * TILE_IMAGES
                act.wait_ge(z_ready, n + 1)
                if g >= 2 and c == 0:
                    act.wait_ge(v_ready, STEPS[g - 1][0])
                dst = zc[0:m, g % 2, c, 0:imgs * POS].rearrange("p (b l) -> p b l", l=POS)[:, :, 0:SEQ]
                src = z_bank(n)[0:m, 0:imgs * SEQ].rearrange("p (b l) -> p b l", l=SEQ)
                nc.scalar.activation(dst, src, ACT.Identity, bias=convw_sb[0:m, c, 3:4],
                                     scale=convw_sb[0:m, c, 2:3]).then_inc(tap2_ready, 1)

            def exponentials(t):
                act.wait_ge(max_ready, t + 1)
                slot_free(act, t)
                for i in range(ORDERS):
                    nc.scalar.activation(
                        staged(t)[:, 0, :, i, :],
                        xs_bank(t)[0:ROWS, i * D:(i + 1) * D].rearrange("p (g d) -> p g d", g=GROUPS),
                        ACT.Exp, bias=nmax[:, t, i:i + 1], accum_out=esum[:, t, i:i + 1]).then_inc(exp_ready, 1)

            def u_evac(p):
                evac_T(bank[2], p, uT_ready, uT_copied, uTA, uTB)

            def load(t):
                act.wait_ge(tok_ready, t - BATCH + 1)
                act.dma_start(xbuf[:, t % BATCH, :], xT[t]).then_inc(x_in[t % BATCH], 16)

            for t in STEPS[2]:
                load(t)
            for p in pairs_of(0):
                u_evac(p)
            for g in range(len(STEPS) + 1):
                for c in range(len(ZCH)):
                    if g < len(STEPS):
                        last_tap(g, c)
                    for p in turned_in(g + 1, c):
                        u_evac(p)
                    for t in back(g - 1, c - 1 if len(STEPS) - 2 <= g < len(STEPS) else c):
                        exponentials(t)
                    for t in at(g + 3, c - 1):
                        load(t)

            def vT_evac(t):
                act.wait_ge(vT_ready, t + 1)
                if t >= 2:
                    act.wait_ge(o_ready, t - 1)
                src = bank[t % 2][0:64, 0:3 * ROWS].rearrange("p (j g l) -> p g j l", g=GROUPS, j=TILE_IMAGES)
                for g, dst in enumerate((vTA[t % 2][0:64], vTA[t % 2][64:128], vTB[t % 2][0:64])):
                    nc.scalar.copy(dst.rearrange("p (j l) -> p j l", j=TILE_IMAGES), src[:, g]).then_inc(vT_copied, 1)

            def n2_evac(p):
                evac_T(bank[2], p, n2T_ready, n2T_copied, n2TA, n2TB)

            def gelu(k):
                act.wait_ge(logit_ready, k + 1)
                n = len(HALVES[k])
                logits = bank[3 if k == 0 else 6][0:ROWS, 0:n * NODES].rearrange("p (t n) -> p t n", n=NODES)
                nc.scalar.activation(act_[k], logits, ACT.Gelu).then_inc(gelu_ready, 1)

            def c_evac(g):
                act.wait_ge(cT_ready, g + 1)
                if g >= 2:
                    act.wait_ge(ffn_ready, 2 * (g - 1))
                n = len(STEPS[g]) * ROWS
                nc.scalar.copy(coefT[0:NODES, g % 2, 0:n], cT_bank(g)[0:NODES, 0:n]).then_inc(cT_copied, 1)

            for t in range(TILES):
                vT_evac(t)
                for p in turned_behind(t):
                    n2_evac(p)
                if LATE - 1 in logits_behind(t):
                    gelu(0)
            for p in range(sum(len(turned_behind(t)) for t in range(TILES)), len(PAIRS)):
                n2_evac(p)
            gelu(1)
            c_evac(0)
            for g in range(LATE):
                if g + 1 < LATE:
                    c_evac(g + 1)
                for p in pairs_of(g):
                    act.wait_ge(ffn_ready, p + 1)
                    nc.scalar.copy(f_sb[p], f_bank(p)[0:ROWS, 0:2 * D]).then_inc(f_copied, 1)
            for g in range(LATE, len(STEPS)):
                c_evac(g)

        @block.vector
        def _(dve):
            def tt(o, a, b, op):
                return nc.vector.tensor_tensor(o, a, b, op)

            nc.vector.memset(warm, 0.0).then_inc(warm_ready, 1)
            nc.vector.memset(uTB[64:128, :, :], 0.0).then_inc(ones_ready, 1)
            dve.wait_ge(ones_ready, 1)
            nc.vector.memset(uTB[64:65, :, :], 1.0).then_inc(ones_ready, 1)
            dve.wait_ge(w_pos, 16)
            tt(pos_sb[:, :], posb_sb[:, 0], posb_sb[:, 1], ALU.add).then_inc(pos_ready, 1)
            dve.wait_ge(pos_ready, 1)

            def moments(t, h_sem, st_sem, mv_sem):
                dve.wait_ge(h_sem, t + 1)
                nc.vector.bn_stats(stats[:, t % 2], h[:, t]).then_inc(st_sem, 1)
                dve.wait_ge(st_sem, t + 1)
                nc.vector.bn_aggr(mv[:, t], stats[:, t % 2]).then_inc(mv_sem, 1)

            def embed(t):
                dve.wait_ge(tok_ready, t + 1)
                tt(h[:, t], tok_bank(t)[0:ROWS, 0:D], pos_sb[:, :], ALU.add).then_inc(h_ready, 1)
                moments(t, h_ready, st_ready, mv_ready)

            def normalise(ts, rstd_sem, out_sem):
                for t in ts:
                    dve.wait_ge(rstd_sem, t // BATCH + 1)
                    nc.vector.tensor_scalar(u[:, t % USLOTS], h[:, t], mv[:, t, 0:1], rstd[:, t:t + 1],
                                            ALU.subtract, ALU.mult).then_inc(out_sem, 1)

            def first_taps(g, c):
                n = len(ZCH) * g + c
                m, imgs = ZCH[c][1], len(STEPS[g]) * TILE_IMAGES
                dst = zc[0:m, g % 2, c, 0:imgs * POS].rearrange("p (b l) -> p b l", l=POS)
                src = z_bank(n)[0:m, 0:imgs * SEQ].rearrange("p (b l) -> p b l", l=SEQ)
                dve.wait_ge(tap2_ready, n + 1)
                nc.vector.scalar_tensor_tensor(dst[:, :, 1:SEQ], src[:, :, 0:SEQ - 1], convw_sb[0:m, c, 1:2],
                                               dst[:, :, 1:SEQ], ALU.mult, ALU.add).then_inc(tap1_ready, 1)
                dve.wait_ge(tap1_ready, n + 1)
                nc.vector.scalar_tensor_tensor(dst[:, :, 2:SEQ], src[:, :, 0:SEQ - 2], convw_sb[0:m, c, 0:1],
                                               dst[:, :, 2:SEQ], ALU.mult, ALU.add).then_inc(zc_ready, 1)

            def maxima_and_v(t):
                dve.wait_ge(xs_ready, t + 1)
                nc.vector.tensor_reduce(nmax[:, t, :], xs_bank(t)[0:ROWS, 0:2 * D].rearrange("p (a d) -> p a d", a=2),
                                        AX_X, ALU.max, negate=True).then_inc(max_ready, 1)
                dve.wait_ge(v_ready, t + 1)
                slot_free(dve, t)
                tt(staged(t)[:, 0, :, ORDERS, :], v_bank(t)[0:ROWS, 0:D].rearrange("p (g d) -> p g d", g=GROUPS),
                   u[:, t % USLOTS].rearrange("p (g d) -> p g d", g=GROUPS), ALU.add).then_inc(vtok_ready, 1)

            def inverse_sums(t):
                dve.wait_ge(exp_ready, 2 * t + 2)
                nc.vector.reciprocal(rsum[:, t, :], esum[:, t, :]).then_inc(rsum_ready, 1)

            f = filt_sb[:, :, :, POS:POS + SEQ]
            done = [0]

            def step(*made):
                for ins in made:
                    ins.then_inc(filt_step, 1)
                    done[0] += 1
                dve.wait_ge(filt_step, done[0])

            def filters_windowed():
                fa = fabs[:, :, :, 0:SEQ]
                dve.wait_ge(w_filt, 16 * 3)
                dve.wait_ge(env_exp, 2)
                step(*(nc.vector.scalar_tensor_tensor(
                    f[:, c], env[:, c, 0:SEQ].unsqueeze(1).broadcast_to([128, ORDERS, SEQ]), fpar_sb[:, c, 1:2],
                    f[:, c], ALU.add, ALU.mult) for c in range(2)))
                step(nc.vector.tensor_scalar(fa.rearrange("p c i l -> p (c i) l"),
                                             f.rearrange("p c i l -> p (c i) l"), -1.0, None, ALU.mult))
                step(tt(fa.rearrange("p c i l -> p (c i) l"), fa.rearrange("p c i l -> p (c i) l"),
                        f.rearrange("p c i l -> p (c i) l"), ALU.max))

            def filters_normed():
                dve.wait_ge(norm_all, 1)
                sums_ = bank[3][0:128, 0:ORDERS * SEQ].rearrange("p (i l) -> p i l", i=ORDERS)
                step(nc.vector.reciprocal(rnorm[:, :, 0:SEQ], sums_))
                step(*(tt(f[:, c], f[:, c], rnorm[:, :, 0:SEQ], ALU.mult) for c in range(2)))
                step(*(tt(f[:, c, :, 0:1], f[:, c, :, 0:1], fpar_sb[:, c, 2:4].unsqueeze(2), ALU.add) for c in range(2)))

            for t in STEPS[0]:
                embed(t)
            filters_windowed()
            normalise(STEPS[0], rstd_ready, u_ready)
            for t in STEPS[1][:2]:
                embed(t)
            filters_normed()
            for t in STEPS[1][2:]:
                embed(t)
            for g in range(len(STEPS) + 1):
                for c in range(len(ZCH)):
                    if g < len(STEPS):
                        first_taps(g, c)
                    for t in at(g + 1, 2 * c - 2) + at(g + 1, 2 * c - 1) if c else []:
                        if t >= USLOTS:
                            dve.wait_ge(vtok_ready, t - USLOTS + 1)
                        normalise([t], rstd_ready, u_ready)
                    for t in back(g - 1, c - 1):
                        inverse_sums(t)
                        if t >= DVE_SCALES:
                            dve.wait_ge(rsum_ready, t + 1)
                            for i in range(ORDERS):
                                e = staged(t)[:, 0, :, i, :]
                                ins = nc.vector.tensor_scalar(e, e, rsum[:, t, i:i + 1], None, ALU.mult)
                            ins.then_inc(gate_last, 1)
                    for t in back(g - 1, c):
                        maxima_and_v(t)
                    for t in at(g + 2, c):
                        embed(t)

            dve.wait_ge(w_late, 16 * 4)
            tt(woutA_sb[:, 0:128], woutA_sb[:, 0:128], ident_sb[:, :], ALU.add).then_inc(wout_ready, 1)
            tt(woutB_sb[0:64, 128:D], woutB_sb[0:64, 128:D], ident_sb[0:64, 0:64], ALU.add).then_inc(wout_ready, 1)
            for k in range(2):
                nc.vector.memset(vTB[k][64:128, :], 0.0).then_inc(wout_ready, 1)
            dve.wait_ge(wout_ready, 4)
            for k in range(2):
                nc.vector.memset(vTB[k][64:65, :], 1.0).then_inc(wout_ready, 1)

            n = 0
            for i in range(ORDERS):
                for k in range(NBLK):
                    dve.wait_ge(y_ready, n + 1)
                    gate = X3[:, 0:IMAGES, i, k * BLK:(k + 1) * BLK].rearrange("p b d -> p d b")
                    v = X3[:, 0:IMAGES, ORDERS, k * BLK:(k + 1) * BLK].rearrange("p b d -> p d b")
                    y = bank[[0, 1, 4, 5][n % 4]][0:ROWS, :].rearrange("p (d b) -> p d b", d=BLK)
                    tt(ytmp[n % 2], y, gate, ALU.mult).then_inc(gated, 1)
                    dve.wait_ge(gated, n + 1)
                    tt(v, v, ytmp[n % 2], ALU.add).then_inc(v_added, 1)
                    n += 1

            def residual(ts):
                for t in ts:
                    dve.wait_ge(o_ready, t + 1)
                    tt(h[:, t], bank[4 + t % 2][0:ROWS, 0:D], h[:, t], ALU.add).then_inc(h2_ready, 1)
                    moments(t, h2_ready, st2_ready, mv2_ready)

            steps = [0]

            FIRST_WALK = LATE * BATCH + BATCH + 2

            def link(ins):
                ins.then_inc(tree, 1)
                steps[0] += 1
                dve.wait_ge(tree, steps[0])

            def walk(k, part):
                ts = HALVES[k]
                a, s, r, c, qq = act_[k], sgn[k], reach[k], coef[k], q[k]
                nl = NODES - 1
                if part == 0:
                    dve.wait_ge(gelu_ready, k + 1)
                    logits = bank[3 if k == 0 else 6][0:ROWS, 0:len(ts) * NODES].rearrange("p (t n) -> p t n", n=NODES)
                    link(nc.vector.tensor_scalar(s, logits[:, :, 0:15], 0.0, None, ALU.is_gt))
                    nc.vector.tensor_copy(r[:, :, 2:3], s[:, :, 0:1])
                    nc.vector.tensor_scalar(r[:, :, 1:2], s[:, :, 0:1], -1.0, 1.0, ALU.mult, ALU.add)
                    link(tt(c[:, :, 2:3], a[:, :, 0:1], s[:, :, 0:1], ALU.mult))
                    link(tt(c[:, :, 1:2], a[:, :, 0:1], c[:, :, 2:3], ALU.subtract))
                elif part < 4:
                    lo, hi = 2 ** part - 1, 2 ** (part + 1) - 1
                    w = hi - lo
                    right = slice(2 * lo + 2, 2 * hi + 1, 2)
                    left = slice(2 * lo + 1, 2 * hi, 2)
                    tt(r[:, :, right], r[:, :, lo:hi], s[:, :, lo:hi], ALU.mult)
                    link(tt(qq[:, :, 0:w], r[:, :, lo:hi], a[:, :, lo:hi], ALU.mult))
                    tt(r[:, :, left], r[:, :, lo:hi], r[:, :, right], ALU.subtract)
                    link(tt(c[:, :, right], qq[:, :, 0:w], s[:, :, lo:hi], ALU.mult))
                    link(tt(c[:, :, left], qq[:, :, 0:w], c[:, :, right], ALU.subtract))
                elif part == 4:
                    nc.vector.tensor_reduce(sums[k][:, :, 0:1], c[:, :, nl:TREE], AX_X, ALU.add)
                    link(nc.vector.tensor_reduce(sums[k][:, :, 1:2], r[:, :, nl:TREE], AX_X, ALU.add))
                    link(nc.vector.tensor_copy(r[:, :, nl:nl + 1], sums[k][:, :, 1:2]))
                    link(tt(last[k], r[:, :, 15:NODES], a[:, :, 15:NODES], ALU.mult))
                else:
                    link(nc.vector.tensor_reduce(sums[k][:, :, 1:2], last[k], AX_X, ALU.add))
                    link(tt(sums[k][:, :, 0:1], sums[k][:, :, 0:1], sums[k][:, :, 1:2], ALU.add))
                    link(nc.vector.scalar_tensor_tensor(c[:, :, nl:nl + 1], a[:, :, nl:nl + 1], 5.0,
                                                        sums[k][:, :, 0:1], ALU.mult, ALU.add))
                    nc.vector.memset(c[:, :, 0:1], 0.0).then_inc(coef_ready, 1)

            for t in range(TILES):
                residual([t])
                if t and t % BATCH == 0:
                    g = t // BATCH - 1
                    if g >= 3:
                        dve.wait_ge(n2T_ready, STEPS[g - 3][-1] // 2 + 1)
                    normalise(STEPS[g], rstd2_ready, n2_ready)
                if t >= FIRST_WALK:
                    walk(0, t - FIRST_WALK)
            normalise(STEPS[-1], rstd2_ready, n2_ready)
            for part in range(TILES - FIRST_WALK, 6):
                walk(0, part)
            for part in range(6):
                walk(1, part)
            for p in range(EARLY, len(PAIRS)):
                dve.wait_ge(ffn_ready, p + 1)
                tt(f_rows(p), f_bank(p)[0:ROWS, 0:2 * D], f_rows(p), ALU.add).then_inc(out_ready, 1)

        @block.tensor
        def _(pe):
            mm = nc.tensor.matmul

            def warm_up(n, width=512, into=2):
                for _ in range(n):
                    mm(bank[into][:, 0:width], warm[:, 0:128], warm[:, 0:width], start=True, stop=True)

            pe.wait_ge(warm_ready, 1)
            warm_up(WARM_START)

            def embed(t):
                pe.wait_ge(x_in[t % BATCH], 16 * (t // BATCH + 1))
                if t >= 2 * BATCH:
                    pe.wait_ge(h_ready, t)
                elif t >= 2:
                    pe.wait_ge(h_ready, t - 1)
                for c in range(KCH):
                    if t == 0 and c == KCH // 2:
                        pe.wait_ge(w_first[1], 16)
                    ins = mm(tok_bank(t)[0:ROWS, 0:D], xbuf[:, t % BATCH, c * ROWS:(c + 1) * ROWS],
                             wproj_sb[:, c, :], start=(c == 0), stop=(c == KCH - 1))
                ins.then_inc(tok_ready, 1)

            def turn(p, src_sem, ready, copied):
                pe.wait_ge(src_sem, 2 * p + 2)
                if p:
                    pe.wait_ge(copied, 2 * p)
                for k in range(2):
                    s = u[:, (2 * p + k) % USLOTS, :]
                    nc.tensor.transpose(bank[2][0:128, k * ROWS:(k + 1) * ROWS], s[:, 0:128], ident_sb[0:ROWS, 0:ROWS])
                for k in range(2):
                    s = u[:, (2 * p + k) % USLOTS, :]
                    ins = nc.tensor.transpose(bank[2][0:64, (2 + k) * ROWS:(3 + k) * ROWS], s[:, 128:D],
                                              ident_sb[0:ROWS, 0:ROWS])
                ins.then_inc(ready, 1)

            def in_project(g, c):
                n = len(ZCH) * g + c
                (c0, m), imgs = ZCH[c], len(STEPS[g]) * TILE_IMAGES
                pe.wait_ge(uT_copied, STEPS[g][-1] + 1)
                if n == THREE:
                    pe.wait_ge(h_ready, TILES)
                elif n >= 2:
                    pe.wait_ge(zc_ready, n - 2 if n > THREE else n - 1)
                dst = z_bank(n)[0:m, 0:imgs * SEQ].rearrange("p (b l) -> p b l", l=SEQ)
                for w, src, rows, a in ((wlinA_sb, uTA, 128, True), (wlinB_sb, uTB, 128, False)):
                    rhs = src[0:rows, g % 2, 0:imgs * POS].rearrange("p (b l) -> p b l", l=POS)[:, :, 0:SEQ]
                    ins = mm(dst, w[0:rows, c0:c0 + m], rhs, start=a, stop=not a)
                ins.then_inc(z_ready, 1)

            def turn_back(t):
                g = t // BATCH
                pe.wait_ge(zc_ready, len(ZCH) * (g + 1))
                if t >= 2:
                    pe.wait_ge(exp_ready, 2 * (t - 1))
                    pe.wait_ge(vtok_ready, t - 1)
                cols = slice((t % BATCH) * ROWS, (t % BATCH + 1) * ROWS)
                for c in range(3):
                    ins = nc.tensor.transpose(xs_bank(t)[0:ROWS, c * 128:(c + 1) * 128],
                                              zc[:, g % 2, c, cols], ident_sb[:, :])
                ins.then_inc(xs_ready, 1)
                nc.tensor.transpose(v_bank(t)[0:ROWS, 0:128], zc[:, g % 2, 3, cols], ident_sb[:, :])
                nc.tensor.transpose(v_bank(t)[0:ROWS, 128:D], zc[0:64, g % 2, 4, cols],
                                    ident_sb[0:64, 0:64]).then_inc(v_ready, 1)

            pe.wait_ge(w_first[0], 16)
            for t in STEPS[0]:
                embed(t)
            embed(STEPS[1][0])
            pe.wait_ge(filt_step, 4)
            pe.wait_ge(const_ready, 3)
            for c in range(2):
                ins = mm(bank[3][0:128, 0:ORDERS * SEQ].rearrange("p (i l) -> p i l", i=ORDERS), ones_sb[:, :],
                         fabs[:, c, :, 0:SEQ], start=(c == 0), stop=(c == 1))
            ins.then_inc(norm_all, 1)
            for t in STEPS[1][1:]:
                embed(t)
            pe.wait_ge(w_rest, 16 * 4)
            pe.wait_ge(ones_ready, 2)
            for p in range(2):
                turn(p, u_ready, uT_ready, uT_copied)
            for g in range(len(STEPS) + 1):
                for c in range(len(ZCH)):
                    if g < len(STEPS):
                        in_project(g, c)
                    for p in turned_in(g + 1, c):
                        turn(p, u_ready, uT_ready, uT_copied)
                    for t in back(g - 1, c):
                        turn_back(t)
                    for t in at(g + 2, c):
                        embed(t)

            warm_up(WARM_MOVE[0])
            for k in range(2):
                pe.wait_ge(gate_last, TILES - DVE_SCALES - 1 + k)
                warm_up(WARM_MOVE[k + 1])
            for k in (3, 0, 1, 2):
                if k == (len(PAIRS) - 1) % 4:
                    warm_up(WARM_MOVE[3])
                pe.wait_ge(moved[k], 16 * sum(len(PARTS) - POOL_PARTS.get(p, 0) for p in range(k, len(PAIRS), 4)))
            pe.wait_ge(moved_pool, 16 * sum(POOL_PARTS.values()))
            n = 0
            for i in range(ORDERS):
                pe.wait_ge(toep_in[i], 16 * GROUPS * POS // COPIES)
                for k in range(NBLK):
                    if n >= 4:
                        pe.wait_ge(gated, n - 3)
                    if i:
                        pe.wait_ge(v_added, k + 1)
                    for j in range(BLK):
                        d = k * BLK + j
                        ins = mm(bank[[0, 1, 4, 5][n % 4]][0:ROWS, j * IMAGES:(j + 1) * IMAGES], toep[i][:, d, :],
                                 X3[:, 0:IMAGES, ORDERS, d], start=True, stop=True)
                    ins.then_inc(y_ready, 1)
                    n += 1

            warm_up(1)
            pe.wait_ge(v_added, n)
            pe.wait_ge(wout_ready, 6)

            def v_turn(t):
                if t >= 2:
                    pe.wait_ge(vT_copied, 3 * (t - 1))
                for j in range(TILE_IMAGES):
                    ins = nc.tensor.transpose(bank[t % 2][0:64, j * ROWS:(j + 1) * ROWS],
                                              X3[:, TILE_IMAGES * t + j, ORDERS, :], ident_sb[0:ROWS, 0:ROWS])
                ins.then_inc(vT_ready, 1)

            def project(t):
                pe.wait_ge(vT_copied, 3 * (t + 1))
                if t >= 2:
                    pe.wait_ge(h2_ready, t - 1)
                mm(bank[4 + t % 2][0:ROWS, 0:D], vTA[t % 2], woutA_sb[:, :], start=True, stop=False)
                mm(bank[4 + t % 2][0:ROWS, 0:D], vTB[t % 2], woutB_sb[:, :], start=False, stop=True).then_inc(o_ready, 1)

            def logits(g):
                pe.wait_ge(n2T_copied, STEPS[g][-1] + 1)
                half = 0 if g < LATE else 1
                for t in STEPS[g]:
                    o = (t - HALVES[half][0]) * NODES
                    dst = bank[3 if half == 0 else 6][0:ROWS, o:o + NODES]
                    c = (t % BATCH) * ROWS
                    mm(dst, n2TA[:, g % 2, c:c + ROWS], wffi_sb[:, 0, :], start=True, stop=False)
                    ins = mm(dst, n2TB[:, g % 2, c:c + ROWS], wffi_sb[:, 1, :], start=False, stop=True)
                if g in (LATE - 1, len(STEPS) - 1):
                    ins.then_inc(logit_ready, 1)

            def c_turn(g):
                half = 0 if g < LATE else 1
                pe.wait_ge(coef_ready, half + 1)
                if g >= 2:
                    pe.wait_ge(cT_copied, g - 1)
                for k, t in enumerate(STEPS[g]):
                    ins = nc.tensor.transpose(cT_bank(g)[0:NODES, k * ROWS:(k + 1) * ROWS],
                                              coef[half][:, t - HALVES[half][0], 0:NODES], ident_sb[0:ROWS, 0:ROWS])
                ins.then_inc(cT_ready, 1)

            def tree_out(g):
                pe.wait_ge(cT_copied, g + 1)
                for k, p in enumerate(pairs_of(g)):
                    if p >= 4:
                        if p - 4 < EARLY:
                            pe.wait_ge(f_copied, p - 3)
                        else:
                            pe.wait_ge(out_ready, p - 3 - EARLY)
                    for m in range(2):
                        ins = mm(f_bank(p)[0:ROWS, m * D:(m + 1) * D],
                                 coefT[:, g % 2, (2 * k + m) * ROWS:(2 * k + m + 1) * ROWS],
                                 wffo_sb[:, :], start=True, stop=True)
                    ins.then_inc(ffn_ready, 1)

            turned = 0
            for t in range(TILES):
                v_turn(t)
                if t:
                    project(t - 1)
                if t == TILES - 1:
                    project(t)
                for p in turned_behind(t):
                    turn(p, n2_ready, n2T_ready, n2T_copied)
                    turned += 1
                for g in logits_behind(t):
                    logits(g)
            for g in range(TILES // BATCH - 1, len(STEPS)):
                for p in pairs_of(g):
                    if p >= turned:
                        warm_up(1, 256, into=7)
                        turn(p, n2_ready, n2T_ready, n2T_copied)
                warm_up(1, 256, into=7)
                logits(g)
            for lot in (range(LATE), range(LATE, len(STEPS))):
                c_turn(lot[0])
                for g in lot:
                    if g + 1 in lot:
                        c_turn(g + 1)
                    tree_out(g)


_SHAPE_OUT = [ROWS, TILES, D]


def _laid_out(i):
    a = {k: np.asarray(v) for k, v in i.items()}
    side = SIDE // PATCH
    f = np.float32
    p = a["x"].reshape(IMAGES, CHANNELS_IN, side, PATCH, side, PATCH).transpose(0, 2, 4, 1, 3, 5)
    x = np.zeros((SLOTS, POS, KDIM), f)
    x[:IMAGES, 1:SEQ] = p.reshape(IMAGES, PATCHES, KDIM)
    xT = x.reshape(TILES, ROWS, KCH, 128).transpose(0, 3, 2, 1).reshape(TILES, 128, KCH * ROWS)
    wproj = a["L0_tok_proj_w"].T.reshape(KCH, 128, D).transpose(1, 0, 2)
    posb = np.zeros((TILE_IMAGES, POS, 2, D), f)
    posb[:, :SEQ, 0] = a["L0_tok_pos_embedding"][0]
    posb[:, 0, 1] = a["L0_tok_cls_token"][0, 0]
    posb[:, 1:SEQ, 1] = a["L0_tok_proj_b"]
    wl = a["L0_attn_W_lin"].T
    wlinB = np.zeros((128, ZC), f)
    wlinB[:64], wlinB[64] = wl[128:], a["L0_attn_b_lin"]
    cw = np.zeros((len(ZCH) * 128, 4), f)
    cw[:ZC, 0:3], cw[:ZC, 3] = a["L0_attn_conv_w"][:, 0], a["L0_attn_conv_b"]
    convw = cw.reshape(len(ZCH), 128, 4).transpose(1, 0, 2)
    wo = a["L0_attn_W_out"].T
    woutB = np.zeros((128, D), f)
    woutB[:64], woutB[64] = wo[128:], a["L0_attn_b_out"]
    filt = np.zeros((2 * 128, ORDERS, 2 * POS), f)
    filt[:D, :, POS:POS + SEQ] = a["L0_attn_h_param"][:, :, :SEQ].transpose(1, 0, 2)
    fpar = np.zeros((2 * 128, 4), f)
    fpar[:D, 0], fpar[:D, 1] = a["L0_attn_alphas"].reshape(D), a["L0_attn_win_b"].reshape(D)
    fpar[:D, 2:4] = a["L0_attn_Bmat"].reshape(ORDERS, D).T
    lags = np.zeros((128, POS), f)
    lags[:, :SEQ] = (np.arange(SEQ, dtype=f) / f(MAXLEN - 1)).astype(f)
    wi = np.zeros((256, NODES), f)
    wi[:D] = a["L0_ffn_weights_in"].T
    wffi = wi.reshape(2, 128, NODES).transpose(1, 0, 2)
    return dict(xT=xT, wproj=wproj, posb=posb.reshape(ROWS, 2, D), wlinA=wl[:128], wlinB=wlinB, convw=convw,
                woutA=wo[:128], woutB=woutB,
                filt=filt.reshape(2, 128, ORDERS, 2 * POS).transpose(1, 0, 2, 3),
                fpar=fpar.reshape(2, 128, 4).transpose(1, 0, 2), lags=lags, ident=np.eye(128, dtype=f), wffi=wffi,
                wffo=np.concatenate([a["L0_ffn_weights_out"], np.zeros((128 - NODES, D), f)]))


def kernel(**inputs):
    import concourse.bacc as bacc
    from concourse.bass_utils import run_bass_kernel_spmd

    nc = bacc.Bacc("TRN2", target_bir_lowering=False, num_devices=1)
    arrays, args = {}, []
    for name, a in _laid_out(inputs).items():
        a = np.ascontiguousarray(a)
        arrays[f"in_{name}"] = a
        args.append(nc.dram_tensor(f"in_{name}", a.shape, F32, kind="ExternalInput").ap())
    out = nc.dram_tensor("out_rows", _SHAPE_OUT, F32, kind="ExternalOutput").ap()
    build(nc, *args, out)
    r = run_bass_kernel_spmd(nc, [arrays], core_ids=[0])
    rows = r.results[0]["out_rows"].reshape(TILE_IMAGES, POS, TILES, D).transpose(2, 0, 1, 3)
    return rows.reshape(SLOTS, POS, D)[:IMAGES, :SEQ]
```
